# Optimizing a Trainium2 kernel written in Bass

```python
import numpy as np
import jax
import jax.numpy as jnp

def _softmax(x, axis=-1):
    return jax.nn.softmax(x, axis=axis)

def _gelu(x):
    return jax.nn.gelu(x, approximate=True)

def _silu(x):
    return jax.nn.silu(x)

def _sigmoid(x):
    return jax.nn.sigmoid(x)

def _layernorm(x, axis=-1, eps=1e-05):
    m = jnp.mean(x, axis=axis, keepdims=True)
    v = jnp.var(x, axis=axis, keepdims=True)
    return (x - m) / jnp.sqrt(v + eps)

def _scatter_add(tgt, idx, src, axis=0):
    return tgt.at[idx].add(src)

def _segment_sum(src, seg, n):
    return jax.ops.segment_sum(src, seg, n)
kernel_name = 'mk_dlrm_tower_d1_rec_r8_d1bef4'

def setup_inputs(seed: int=0):
    np.random.seed(seed)
    _w = jnp.asarray

    def _rec_inputs():
        import jax
        import jax.numpy as jnp
        _tk = jax.random.key(seed)
        dense_ctx = jax.random.normal(jax.random.fold_in(_tk, 190), (2048, 16), jnp.float32)
        ids = jnp.stack([jax.random.randint(jax.random.fold_in(_tk, 200 + f), (2048,), 0, v, jnp.int32) for f, v in enumerate([1250, 1250, 125000, 125000, 1000, 1250, 1250, 1000, 1250, 1000, 1250, 12500, 1250, 12500, 1250, 125000, 1250, 1250, 1250, 1000, 125000, 12500, 125000, 12500, 1000, 1250])], axis=1)
        tbl_0 = 0.05 * jax.random.normal(jax.random.fold_in(_tk, 500 + 0), (1250, 32), jnp.float32)
        tbl_1 = 0.05 * jax.random.normal(jax.random.fold_in(_tk, 500 + 1), (1250, 32), jnp.float32)
        tbl_2 = 0.05 * jax.random.normal(jax.random.fold_in(_tk, 500 + 2), (125000, 32), jnp.float32)
        tbl_3 = 0.05 * jax.random.normal(jax.random.fold_in(_tk, 500 + 3), (125000, 32), jnp.float32)
        tbl_4 = 0.05 * jax.random.normal(jax.random.fold_in(_tk, 500 + 4), (1000, 32), jnp.float32)
        tbl_5 = 0.05 * jax.random.normal(jax.random.fold_in(_tk, 500 + 5), (1250, 32), jnp.float32)
        tbl_6 = 0.05 * jax.random.normal(jax.random.fold_in(_tk, 500 + 6), (1250, 32), jnp.float32)
        tbl_7 = 0.05 * jax.random.normal(jax.random.fold_in(_tk, 500 + 7), (1000, 32), jnp.float32)
        tbl_8 = 0.05 * jax.random.normal(jax.random.fold_in(_tk, 500 + 8), (1250, 32), jnp.float32)
        tbl_9 = 0.05 * jax.random.normal(jax.random.fold_in(_tk, 500 + 9), (1000, 32), jnp.float32)
        tbl_10 = 0.05 * jax.random.normal(jax.random.fold_in(_tk, 500 + 10), (1250, 32), jnp.float32)
        tbl_11 = 0.05 * jax.random.normal(jax.random.fold_in(_tk, 500 + 11), (12500, 32), jnp.float32)
        tbl_12 = 0.05 * jax.random.normal(jax.random.fold_in(_tk, 500 + 12), (1250, 32), jnp.float32)
        tbl_13 = 0.05 * jax.random.normal(jax.random.fold_in(_tk, 500 + 13), (12500, 32), jnp.float32)
        tbl_14 = 0.05 * jax.random.normal(jax.random.fold_in(_tk, 500 + 14), (1250, 32), jnp.float32)
        tbl_15 = 0.05 * jax.random.normal(jax.random.fold_in(_tk, 500 + 15), (125000, 32), jnp.float32)
        tbl_16 = 0.05 * jax.random.normal(jax.random.fold_in(_tk, 500 + 16), (1250, 32), jnp.float32)
        tbl_17 = 0.05 * jax.random.normal(jax.random.fold_in(_tk, 500 + 17), (1250, 32), jnp.float32)
        tbl_18 = 0.05 * jax.random.normal(jax.random.fold_in(_tk, 500 + 18), (1250, 32), jnp.float32)
        tbl_19 = 0.05 * jax.random.normal(jax.random.fold_in(_tk, 500 + 19), (1000, 32), jnp.float32)
        tbl_20 = 0.05 * jax.random.normal(jax.random.fold_in(_tk, 500 + 20), (125000, 32), jnp.float32)
        tbl_21 = 0.05 * jax.random.normal(jax.random.fold_in(_tk, 500 + 21), (12500, 32), jnp.float32)
        tbl_22 = 0.05 * jax.random.normal(jax.random.fold_in(_tk, 500 + 22), (125000, 32), jnp.float32)
        tbl_23 = 0.05 * jax.random.normal(jax.random.fold_in(_tk, 500 + 23), (12500, 32), jnp.float32)
        tbl_24 = 0.05 * jax.random.normal(jax.random.fold_in(_tk, 500 + 24), (1000, 32), jnp.float32)
        tbl_25 = 0.05 * jax.random.normal(jax.random.fold_in(_tk, 500 + 25), (1250, 32), jnp.float32)
        _rk = jax.random.fold_in(_tk, 7)
        W_top1 = 0.0606339 * jax.random.normal(jax.random.fold_in(_tk, 801), (272, 512), jnp.float32)
        W_top2 = 0.0441942 * jax.random.normal(jax.random.fold_in(_tk, 802), (512, 256), jnp.float32)
        W_top3 = 0.0625 * jax.random.normal(jax.random.fold_in(_tk, 803), (256, 1), jnp.float32)
        b_top1 = jnp.zeros((512,), jnp.float32)
        b_top2 = jnp.zeros((256,), jnp.float32)
        return (dense_ctx, ids, tbl_0, tbl_1, tbl_2, tbl_3, tbl_4, tbl_5, tbl_6, tbl_7, tbl_8, tbl_9, tbl_10, tbl_11, tbl_12, tbl_13, tbl_14, tbl_15, tbl_16, tbl_17, tbl_18, tbl_19, tbl_20, tbl_21, tbl_22, tbl_23, tbl_24, tbl_25, W_top1, b_top1, W_top2, b_top2, W_top3)
    dense_ctx, ids, tbl_0, tbl_1, tbl_2, tbl_3, tbl_4, tbl_5, tbl_6, tbl_7, tbl_8, tbl_9, tbl_10, tbl_11, tbl_12, tbl_13, tbl_14, tbl_15, tbl_16, tbl_17, tbl_18, tbl_19, tbl_20, tbl_21, tbl_22, tbl_23, tbl_24, tbl_25, W_top1, b_top1, W_top2, b_top2, W_top3 = _rec_inputs()

    def _L0_rec_setup():
        import jax, jax.numpy as jnp
        import numpy as np
        M_FIELDS = 26
        H1 = 128
        H2 = 128
        BATCH = 256
        EMB_K = 32

        def _cin_layer(x_prev, x0, W, b):
            return jnp.einsum('bik,bjk,hij->bhk', x_prev, x0, W) + b[None, :, None]
        key = jax.random.key(seed)
        k0, k1, k2, k3, k4 = jax.random.split(key, 5)
        inputs = jax.random.normal(k0, (BATCH, M_FIELDS, EMB_K), dtype=jnp.float32)
        W1 = jax.random.normal(k1, (H1, M_FIELDS, M_FIELDS), dtype=jnp.float32) * 0.05
        b1 = jax.random.normal(k2, (H1,), dtype=jnp.float32) * 0.05
        W2 = jax.random.normal(k3, (H2, H1, M_FIELDS), dtype=jnp.float32) * 0.05
        b2 = jax.random.normal(k4, (H2,), dtype=jnp.float32) * 0.05
        return {'inputs': inputs, 'W1': W1, 'b1': b1, 'W2': W2, 'b2': b2}
    _L0_rec_all = _L0_rec_setup()
    _L0_rec_in = {k: v for k, v in _L0_rec_all.items() if k in ('W1', 'b1', 'W2', 'b2')}
    del _L0_rec_all
    return {'dense_ctx': dense_ctx, 'ids': ids, 'tbl_0': tbl_0, 'tbl_1': tbl_1, 'tbl_2': tbl_2, 'tbl_3': tbl_3, 'tbl_4': tbl_4, 'tbl_5': tbl_5, 'tbl_6': tbl_6, 'tbl_7': tbl_7, 'tbl_8': tbl_8, 'tbl_9': tbl_9, 'tbl_10': tbl_10, 'tbl_11': tbl_11, 'tbl_12': tbl_12, 'tbl_13': tbl_13, 'tbl_14': tbl_14, 'tbl_15': tbl_15, 'tbl_16': tbl_16, 'tbl_17': tbl_17, 'tbl_18': tbl_18, 'tbl_19': tbl_19, 'tbl_20': tbl_20, 'tbl_21': tbl_21, 'tbl_22': tbl_22, 'tbl_23': tbl_23, 'tbl_24': tbl_24, 'tbl_25': tbl_25, 'W_top1': W_top1, 'b_top1': b_top1, 'W_top2': W_top2, 'b_top2': b_top2, 'W_top3': W_top3, 'L0_rec_W1': _L0_rec_in['W1'], 'L0_rec_b1': _L0_rec_in['b1'], 'L0_rec_W2': _L0_rec_in['W2'], 'L0_rec_b2': _L0_rec_in['b2']}

def reference(dense_ctx, ids, tbl_0, tbl_1, tbl_2, tbl_3, tbl_4, tbl_5, tbl_6, tbl_7, tbl_8, tbl_9, tbl_10, tbl_11, tbl_12, tbl_13, tbl_14, tbl_15, tbl_16, tbl_17, tbl_18, tbl_19, tbl_20, tbl_21, tbl_22, tbl_23, tbl_24, tbl_25, W_top1, b_top1, W_top2, b_top2, W_top3, L0_rec_W1, L0_rec_b1, L0_rec_W2, L0_rec_b2):
    import jax
    import jax.numpy as jnp

    def _L0_rec_ref(inputs, W1, b1, W2, b2):
        import jax, jax.numpy as jnp
        import numpy as np
        M_FIELDS = 26
        H1 = 128
        H2 = 128
        BATCH = 256
        EMB_K = 32

        def _cin_layer(x_prev, x0, W, b):
            return jnp.einsum('bik,bjk,hij->bhk', x_prev, x0, W) + b[None, :, None]
        x1 = _cin_layer(inputs, inputs, W1, b1)
        x2 = _cin_layer(x1, inputs, W2, b2)
        res = jnp.concatenate([x1, x2], axis=1)
        return jnp.sum(res, axis=-1)
    e = jnp.stack([tbl_0[ids[:, 0]], tbl_1[ids[:, 1]], tbl_2[ids[:, 2]], tbl_3[ids[:, 3]], tbl_4[ids[:, 4]], tbl_5[ids[:, 5]], tbl_6[ids[:, 6]], tbl_7[ids[:, 7]], tbl_8[ids[:, 8]], tbl_9[ids[:, 9]], tbl_10[ids[:, 10]], tbl_11[ids[:, 11]], tbl_12[ids[:, 12]], tbl_13[ids[:, 13]], tbl_14[ids[:, 14]], tbl_15[ids[:, 15]], tbl_16[ids[:, 16]], tbl_17[ids[:, 17]], tbl_18[ids[:, 18]], tbl_19[ids[:, 19]], tbl_20[ids[:, 20]], tbl_21[ids[:, 21]], tbl_22[ids[:, 22]], tbl_23[ids[:, 23]], tbl_24[ids[:, 24]], tbl_25[ids[:, 25]]], axis=1)
    z = _L0_rec_ref(e, L0_rec_W1, L0_rec_b1, L0_rec_W2, L0_rec_b2)
    z = z.reshape(z.shape[0], -1)
    h = jnp.concatenate([z, dense_ctx], axis=1)
    h = jnp.maximum(h @ W_top1 + b_top1, 0.0)
    h = jnp.maximum(h @ W_top2 + b_top2, 0.0)
    y = h @ W_top3
    return y

_drawn_inputs = setup_inputs


def setup_inputs(seed=0):
    import zlib

    import numpy as np

    out = dict(_drawn_inputs(seed))
    spreads = {'b_top1': (0.0, 2.0), 'b_top2': (0.0, 0.8)}
    factors = {'tbl_0': 8.0,
     'tbl_1': 8.0,
     'tbl_2': 8.0,
     'tbl_3': 8.0,
     'tbl_4': 8.0,
     'tbl_5': 8.0,
     'tbl_6': 8.0,
     'tbl_7': 8.0,
     'tbl_8': 8.0,
     'tbl_9': 8.0,
     'tbl_10': 8.0,
     'tbl_11': 8.0,
     'tbl_12': 8.0,
     'tbl_13': 8.0,
     'tbl_14': 8.0,
     'tbl_15': 8.0,
     'tbl_16': 8.0,
     'tbl_17': 8.0,
     'tbl_18': 8.0,
     'tbl_19': 8.0,
     'tbl_20': 8.0,
     'tbl_21': 7.662,
     'tbl_22': 8.0,
     'tbl_23': 8.0,
     'tbl_24': 8.0,
     'tbl_25': 8.0,
     'L0_rec_W1': 8.0,
     'L0_rec_W2': 4.091,
     'dense_ctx': 5.559}
    for name, (base, spread) in spreads.items():
        noise = np.random.default_rng([zlib.crc32(name.encode()), seed]).standard_normal(out[name].shape)
        drawn = base * np.exp(spread * noise) if base else spread * noise
        out[name] = jnp.asarray(drawn.astype(out[name].dtype))
    for name, factor in factors.items():
        out[name] = (out[name] * factor).astype(out[name].dtype)
    return out
```

```python
from contextlib import ExitStack

import concourse.bass as bass
from concourse import mybir

fp32 = mybir.dt.float32
int32 = mybir.dt.int32
ALU = mybir.AluOpType
ACT = mybir.ActivationFunctionType

NP = 128
B, F, K = 2048, 26, 32
H = 128
ND = 16
N1, N2 = 512, 256
TILES = B // NP
Q = NP // K
GROUPS = NP // Q
HALF = GROUPS // 2
UNIT = 4
UNITS = GROUPS // UNIT
BANK = 512

FIRST = [0, 15, 21]
LAST = [15, 21, 26]


def tri(r):
    return r * (r + 1) // 2


def chunk(r):
    return next(c for c in range(3) if r < LAST[c])


START = [0, 1 + tri(FIRST[1]), 1 + tri(FIRST[2])]
WIDTH = [1 + tri(15), tri(21) - tri(15), tri(26) - tri(21)]
ROWS = max(WIDTH)
PAIRS = START[2] + ROWS
SLOTS = [F + 1 - FIRST[c] for c in range(3)]
SLOT0 = [0, SLOTS[0], SLOTS[0] + SLOTS[1]]
NSLOT = sum(SLOTS)
ONE = F

TOP = F - FIRST[1]
XROWS = FIRST[2]
XSLOT0 = [0, TOP, 2 * TOP]
NXSLOT = 2 * TOP + F - FIRST[2]


def column(r):
    return 1 + tri(r) - START[chunk(r)]


def build(nc, dense_ctx, ids, tables, W_top1, b_top1, W_top2, b_top2, W_top3, W1, b1, W2, b2, out):
    ctx = ExitStack()
    with ctx:
        def sb(name, shape, dt=fp32):
            return ctx.enter_context(nc.sbuf_tensor(name, shape, dt))

        def sem(name):
            return ctx.enter_context(nc.semaphore(name))

        idx = [sb(f"idx{n}", [NP, F], int32) for n in range(2)]
        emb = [sb(f"emb{n}", [NP, F * K]) for n in range(2)]
        embT = [sb(f"embT{n}", [NP, F * GROUPS]) for n in range(2)]
        diag = sb("diag", [NP, 2, GROUPS, Q, F + 1])
        pair_area = sb("pair_area", [NP, 2 * HALF * PAIRS])
        pairs = pair_area[:, :].rearrange("p (n g c) -> p n g c", n=2, g=HALF)
        t_area = sb("t_area", [NP, 2 * NSLOT * NP])
        tsum = t_area[:, :].rearrange("p (n s b) -> p n s b", n=2, s=NSLOT)
        v = sb("v", [NP, NSLOT, H])
        ident = sb("ident", [NP, NP])
        top1 = sb("top1", [NP, 2, N1])
        top1d = sb("top1d", [K, N1])
        top2 = sb("top2", [NP, N1 // NP, N2])
        top3 = sb("top3", [NP, N2 // NP])
        bias2 = sb("bias2", [NP, N2 // NP])
        b2row = sb("b2row", [1, H])
        denseT = sb("denseT", [K, B])
        z = sb("z", [NP, 2, NP])
        h1 = sb("h1", [NP, N1 // NP, NP])
        h2 = sb("h2", [NP, N2 // NP, NP])
        y = sb("y", [1, B])

        at = 0
        moved = pair_area[:, at:at + XROWS * TOP * F].rearrange("p (x m z) -> p x m z", x=XROWS, m=TOP)
        at += XROWS * TOP * F
        w2raw = pair_area[:, at:at + H * F].rearrange("p (i m) -> p i m", m=F)
        at += H * F
        dense = pair_area[:, at:at + TILES * K].rearrange("p (t c) -> p t c", c=K)
        at += TILES * K
        dense_q = pair_area[:, at:at + TILES * K].rearrange("p (t c) -> p t c", c=K)
        assert at + TILES * K <= 2 * HALF * PAIRS
        at = 0
        w2T = t_area[:, at:at + F * H].rearrange("p (m h) -> p m h", h=H)
        at += F * H
        extra = t_area[:, at:at + NXSLOT * ROWS].rearrange("p (s c) -> p s c", c=ROWS)
        at += NXSLOT * ROWS
        w1p = t_area[:, at:at + PAIRS - 1]
        at += PAIRS - 1
        w1top = t_area[:, at:at + TOP * F].rearrange("p (m z) -> p m z", m=TOP)
        at += TOP * F
        w1raw = t_area[:, at:at + F * F].rearrange("p (r c) -> p r c", c=F)
        assert at + F * F <= 2 * NSLOT * NP

        psum = ctx.enter_context(nc.psum_tensor("psum", [NP, 8, BANK], fp32))
        z_ps, h1_ps, h2_ps, y_ps = (psum[:, n, :] for n in range(4, 8))

        w1_in, w2_in, b1_in = sem("w1_in"), sem("w2_in"), sem("b1_in")
        dense_in, top_in = sem("dense_in"), sem("top_in")
        idx_in = [sem(f"idx_in{n}") for n in range(2)]
        gathered = [sem(f"gathered{n}") for n in range(2)]
        ident_zero, ident_ready = sem("ident_zero"), sem("ident_ready")
        dense_pad = sem("dense_pad")
        dve_own = sem("dve_own")
        sym_ready = sem("sym_ready")
        prep_full = sem("prep_full")
        prep_out = sem("prep_out")
        extra_ready = sem("extra_ready")
        consts_ready = sem("consts_ready")
        embT_ready, diag_ready = sem("embT_ready"), sem("diag_ready")
        pairs_ready = sem("pairs_ready")
        t_full, t_out = sem("t_full"), sem("t_out")
        z_full, z_out = sem("z_full"), sem("z_out")
        h1_full, h1_out = sem("h1_full"), sem("h1_out")
        h2_full, h2_out = sem("h2_full"), sem("h2_out")
        y_full, y_out = sem("y_full"), sem("y_out")
        stored = sem("stored")

        ROWS_IN = 16 * F

        w2T_jobs = [range(m, min(m + 4, F)) for m in range(0, F, 4)]
        v_jobs = [(c, range(s, min(s + 4, SLOTS[c]))) for c in range(3) for s in range(0, SLOTS[c], 4)]
        AFTER_W2T = len(w2T_jobs)
        AFTER_MOVED = AFTER_W2T + XROWS
        PREPS = AFTER_MOVED + len(v_jobs)

        def prep_bank(n):
            return psum[:, 4 + n % 4, :]

        block = ctx.enter_context(nc.Block())

        @block.sync
        def _(eng):
            def load_idx(t, n):
                eng.dma_start(idx[n][:, :], ids[bass.ts(t, NP), :]).then_inc(idx_in[n], 16)

            load_idx(0, 0)
            load_idx(1, 1)
            eng.dma_start(w2raw.rearrange("p i m -> p (i m)"), W2.rearrange("h i m -> h (i m)")).then_inc(w2_in, 16)
            eng.dma_start(w1raw.rearrange("p r c -> p (r c)"), W1.rearrange("h r c -> h (r c)")).then_inc(w1_in, 16)
            eng.dma_start(w1p[:, 0:1], b1.rearrange("(h o) -> h o", o=1)).then_inc(b1_in, 16)
            eng.wait_ge(dense_pad, 1)
            eng.dma_start(dense[:, :, 0:ND], dense_ctx.rearrange("(t p) c -> p t c", p=NP)).then_inc(dense_in, 16)
            eng.dma_start(top1[:, :, :], W_top1[0:2 * H, :].rearrange("(a p) n -> p a n", p=NP)).then_inc(top_in, 16)
            eng.dma_start(top1d[0:ND, :], W_top1[2 * H:2 * H + ND, :]).then_inc(top_in, 16)
            eng.dma_start(top1d[ND:ND + 1, :], b_top1.rearrange("(o n) -> o n", o=1)).then_inc(top_in, 16)
            eng.dma_start(top2[:, :, :], W_top2.rearrange("(a p) n -> p a n", p=NP)).then_inc(top_in, 16)
            eng.dma_start(top3[:, :], W_top3.rearrange("(p a) o -> p (a o)", p=NP)).then_inc(top_in, 16)
            eng.dma_start(bias2[:, :], b_top2.rearrange("(p a) -> p a", p=NP)).then_inc(top_in, 16)
            eng.dma_start(b2row[:, :], b2.rearrange("(o n) -> o n", o=1)).then_inc(top_in, 16)
            with eng.Fori(1, TILES // 2) as i:
                for n in range(2):
                    eng.wait_ge(gathered[n], ROWS_IN * i)
                    load_idx(2 * i + n, n)
            eng.wait_ge(y_out, TILES)
            eng.dma_start(out.rearrange("b o -> o b"), y[:, :]).then_inc(stored, 16)
            eng.wait_ge(stored, 16)

        LOADS_TOP = 7

        @block.gpsimd
        def _(eng):
            eng.memset(ident[:, :], 0.0).then_inc(ident_zero, 1)
            eng.wait_ge(ident_zero, 1)
            eng.affine_select(out=ident[:, :], in_=ident[:, :], compare_op=ALU.not_equal, fill=1.0, base=0,
                              pattern=[[-1, NP]], channel_multiplier=1).then_inc(ident_ready, 1)

            def gather(i, n):
                eng.wait_ge(idx_in[n], 16 * i + 16)
                eng.nop(nofuse=True)
                for f in range(F):
                    eng.indirect_dma_start(
                        emb[n][:, f * K:(f + 1) * K], None, tables[f],
                        bass.IndirectOffsetOnAxis(ap=idx[n][:, f:f + 1], axis=0),
                    ).then_inc(gathered[n], 16)

            gather(0, 0)
            gather(0, 1)
            with eng.Fori(1, TILES // 2) as i:
                for n in range(2):
                    eng.wait_ge(embT_ready, 2 * i + n - 1)
                    gather(i, n)

        @block.vector
        def _(eng):
            own = 0

            nc.vector.memset(dense, 1.0).then_inc(dense_pad, 1)
            nc.vector.memset(extra, 0.0)
            nc.vector.memset(diag[:, :, :, :, :], 0.0).then_inc(dve_own, 1)
            own += 1
            eng.wait_ge(dve_own, own)
            for q in range(Q):
                part = slice(K * q, K * q + K)
                nc.vector.memset(diag[part, :, :, q, ONE], 1.0)

            eng.wait_ge(w1_in, 16)
            diagonal = w1raw.rearrange("p r c -> p (r c)")[:, 0:F * F:F + 1]
            nc.vector.tensor_scalar(diagonal, diagonal, 0.5, None, ALU.mult).then_inc(dve_own, 1)
            own += 1
            eng.wait_ge(dve_own, own)
            w1t = w1raw.rearrange("p r c -> p c r")
            nc.vector.tensor_tensor(w1top, w1raw[:, FIRST[1]:F, :], w1t[:, FIRST[1]:F, :], ALU.add)
            for r in range(F):
                at = 1 + tri(r)
                last = nc.vector.tensor_tensor(w1p[:, at:at + r + 1], w1raw[:, r, 0:r + 1], w1t[:, r, 0:r + 1], ALU.add)
            last.then_inc(sym_ready, 1)

            eng.wait_ge(dense_in, 16)
            nc.vector.transpose(dense_q.rearrange("p t c -> p (t c)"), dense.rearrange("p t c -> p (t c)"))\
                .then_inc(dve_own, 1)
            own += 1
            eng.wait_ge(dve_own, own)
            for q in range(Q):
                dst = denseT[0:ND + 1, :].rearrange("p (t q g) -> p q t g", q=Q, g=GROUPS)[:, q]
                last = nc.vector.tensor_copy(dst, dense_q[K * q:K * q + ND + 1, :, :])
            last.then_inc(consts_ready, 1)

            eng.wait_ge(prep_out, AFTER_MOVED)
            halves = bass.AP(moved.tensor, moved.offset, [list(moved.ap[0]), [TOP * F + 1, XROWS], [F, TOP]])
            nc.vector.tensor_scalar(halves, halves, 0.5, None, ALU.mult).then_inc(dve_own, 1)
            own += 1
            eng.wait_ge(dve_own, own)
            by_x = moved.rearrange("p x m z -> p m z x")
            for r in range(F):
                c = chunk(r)
                at = column(r)
                if c < 2:
                    m0 = LAST[c]
                    s0 = XSLOT0[c] + m0 - FIRST[1]
                    s1 = XSLOT0[c] + TOP
                    last = nc.vector.tensor_tensor(extra[:, s0:s1, at:at + r + 1],
                                                   moved[:, r, m0 - FIRST[1]:TOP, 0:r + 1],
                                                   by_x[:, m0 - FIRST[1]:TOP, r, 0:r + 1], ALU.add)
                if c > 0:
                    base = XSLOT0[c] - max(FIRST[1], FIRST[c])
                    last = nc.vector.tensor_copy(extra[:, base + r:base + LAST[c], at:at + FIRST[c]],
                                                 by_x[:, r - FIRST[1]:LAST[c] - FIRST[1], r, 0:FIRST[c]])
            last.then_inc(extra_ready, 1)

            eng.wait_ge(extra_ready, 1)
            nc.vector.memset(pairs[:, :, :, 0:1], 1.0)
            nc.vector.memset(pairs[:, :, :, PAIRS - 1:PAIRS], 1.0)

            def tile(t, i, n):
                eng.wait_ge(gathered[n], ROWS_IN * i + ROWS_IN)
                if not (isinstance(t, int) and t < 2):
                    eng.wait_ge(diag_ready, t - 1)
                nc.vector.transpose(embT[n][:, :], emb[n][:, :]).then_inc(embT_ready, 1)
                eng.wait_ge(embT_ready, t + 1)
                e = embT[n][:, :].rearrange("p (m g) -> p g m", g=GROUPS)
                for half in range(2):
                    if not (isinstance(t, int) and t < 1):
                        eng.wait_ge(t_full, UNITS * t - UNITS + (UNITS // 2) * (half + 1))
                    g = slice(HALF * half, HALF * half + HALF)
                    for r in range(F):
                        at = 1 + tri(r)
                        last = nc.vector.tensor_tensor(pairs[:, half, :, at:at + r + 1], e[:, g, 0:r + 1],
                                                       e[:, g, r:r + 1].broadcast_to([NP, HALF, r + 1]), ALU.mult)
                    last.then_inc(pairs_ready, 1)

            tile(0, 0, 0)
            tile(1, 0, 1)
            with eng.Fori(1, TILES // 2) as i:
                for n in range(2):
                    tile(2 * i + n, i, n)

        @block.scalar
        def _(eng):
            for n, ms in enumerate(w2T_jobs):
                eng.wait_ge(prep_full, n + 1)
                nc.scalar.copy(w2T[:, ms[0]:ms[-1] + 1, :].rearrange("p m h -> p (m h)"),
                               prep_bank(n)[:, 0:len(ms) * H]).then_inc(prep_out, 1)
            for x in range(XROWS):
                n = AFTER_W2T + x
                eng.wait_ge(prep_full, n + 1)
                nc.scalar.copy(moved[:, x].rearrange("p m z -> p (m z)"), prep_bank(n)[:, 0:TOP * F])\
                    .then_inc(prep_out, 1)
            for n, (c, ss) in enumerate(v_jobs, AFTER_MOVED):
                eng.wait_ge(prep_full, n + 1)
                s = SLOT0[c] + ss[0]
                nc.scalar.copy(v[0:WIDTH[c], s:s + len(ss), :].rearrange("p s h -> p (s h)"),
                               prep_bank(n)[0:WIDTH[c], 0:len(ss) * H]).then_inc(prep_out, 1)

            def fill_diag(t, n):
                eng.wait_ge(embT_ready, t + 1)
                if not (isinstance(t, int) and t < 2):
                    eng.wait_ge(t_full, UNITS * t - UNITS)
                for q in range(Q):
                    part = slice(K * q, K * q + K)
                    last = nc.scalar.copy(diag[part, n, :, q, 0:F],
                                          embT[n][part, :].rearrange("p (m g) -> p g m", g=GROUPS))
                last.then_inc(diag_ready, 1)

            def unit_out(t, n, u):
                if u == 0 and not (isinstance(t, int) and t < 2):
                    eng.wait_ge(z_full, t - 1)
                eng.wait_ge(t_full, UNITS * t + u + 1)
                src = psum[0:ROWS, 2 * (u % 2):2 * (u % 2) + 2, :].rearrange("p a (b c) -> p (a b) c", b=2)
                src = src[:, :, 0:Q * NSLOT].rearrange("p g (q s) -> p g q s", q=Q)
                dst = tsum[0:ROWS, n].rearrange("p s (q g) -> p g q s", q=Q)[:, UNIT * u:UNIT * u + UNIT]
                nc.scalar.copy(dst, src).then_inc(t_out, 1)

            def z_move(t):
                if not (isinstance(t, int) and t < 1):
                    eng.wait_ge(h1_full, t)
                eng.wait_ge(z_full, t + 1)
                nc.scalar.copy(z[:, :, :].rearrange("p a b -> p (a b)"), z_ps[:, 0:2 * NP]).then_inc(z_out, 1)

            def h1_move(t):
                if not (isinstance(t, int) and t < 1):
                    eng.wait_ge(h2_full, t)
                eng.wait_ge(h1_full, t + 1)
                nc.scalar.activation(h1[:, :, :].rearrange("p a b -> p (a b)"), h1_ps, ACT.Relu).then_inc(h1_out, 1)

            def h2_move(t):
                if not (isinstance(t, int) and t < 1):
                    eng.wait_ge(y_full, t)
                eng.wait_ge(h2_full, t + 1)
                for a in range(N2 // NP):
                    last = nc.scalar.activation(h2[:, a, :], h2_ps[:, a * NP:(a + 1) * NP], ACT.Relu,
                                                bias=bias2[:, a:a + 1])
                last.then_inc(h2_out, 1)

            def y_move(t):
                eng.wait_ge(y_full, t + 1)
                nc.scalar.copy(y[0:1, bass.ts(t, NP)], y_ps[0:1, 0:NP]).then_inc(y_out, 1)

            def step(t, n):
                known = isinstance(t, int)
                if not known or t < TILES:
                    for u in range(UNITS // 2):
                        unit_out(t, n, u)
                if not known or t >= 2:
                    h1_move(t - 2)
                if not known or t < TILES:
                    for u in range(UNITS // 2, UNITS):
                        unit_out(t, n, u)
                if not known or t >= 2:
                    h2_move(t - 2)
                if not known or t + 1 < TILES:
                    fill_diag(t + 1, 1 - n)
                if not known or 1 <= t <= TILES:
                    z_move(t - 1)
                if not known or t >= 2:
                    y_move(t - 2)

            eng.wait_ge(consts_ready, 1)
            eng.wait_ge(top_in, 16 * LOADS_TOP)
            fill_diag(0, 0)
            for t in range(4):
                step(t, t % 2)
            with eng.Fori(2, TILES // 2 - 1) as i:
                for n in range(2):
                    step(2 * i + n, n)
            for t in range(TILES - 2, TILES + 2):
                step(t, t % 2)

        @block.tensor
        def _(eng):
            def free_bank(n):
                if n >= 4:
                    eng.wait_ge(prep_out, n - 3)

            eng.wait_ge(ident_ready, 1)
            eng.wait_ge(w2_in, 16)
            for n, ms in enumerate(w2T_jobs):
                free_bank(n)
                for a, m in enumerate(ms):
                    last = nc.tensor.transpose(prep_bank(n)[:, a * H:(a + 1) * H], w2raw[:, :, m], ident[:, :])
                last.then_inc(prep_full, 1)
            eng.wait_ge(sym_ready, 1)
            for x in range(XROWS):
                n = AFTER_W2T + x
                eng.wait_ge(prep_out, max(n - 3, x // 4 + 1))
                nc.tensor.matmul(prep_bank(n)[:, 0:TOP * F], w2T[:, x, :], w1top.rearrange("p m z -> p (m z)"),
                                 start=True, stop=True).then_inc(prep_full, 1)
            eng.wait_ge(b1_in, 16)
            eng.wait_ge(extra_ready, 1)
            for n, (c, ss) in enumerate(v_jobs, AFTER_MOVED):
                free_bank(n)
                for a, s in enumerate(ss):
                    dst = prep_bank(n)[0:WIDTH[c], a * H:(a + 1) * H]
                    own = w1p[:, START[c]:START[c] + WIDTH[c]]
                    m = FIRST[c] + s
                    if m == ONE:
                        last = nc.tensor.matmul(dst, own, ident[:, :], start=True, stop=True)
                    elif m < FIRST[1]:
                        last = nc.tensor.matmul(dst, own, w2T[:, m, :], start=True, stop=True)
                    else:
                        nc.tensor.matmul(dst, own, w2T[:, m, :], start=True, stop=False)
                        x = XSLOT0[c] + m - max(FIRST[1], FIRST[c])
                        last = nc.tensor.matmul(dst, extra[:, x, 0:WIDTH[c]], ident[:, :], start=False, stop=True)
                last.then_inc(prep_full, 1)

            def t_units(t, n, half):
                eng.wait_ge(pairs_ready, 2 * t + half + 1)
                if half == 0:
                    eng.wait_ge(diag_ready, t + 1)
                for u in range(half * UNITS // 2, (half + 1) * UNITS // 2):
                    if not (isinstance(t, int) and UNITS * t + u < 2):
                        eng.wait_ge(t_out, UNITS * t + u - 1)
                    for j in range(UNIT):
                        g = UNIT * u + j
                        dst = psum[0:ROWS, 2 * (u % 2) + j // 2, (j % 2) * (BANK // 2):(j % 2) * (BANK // 2) + Q * NSLOT]
                        dst = dst.rearrange("p (q s) -> p q s", q=Q)
                        for c in range(3):
                            last = nc.tensor.matmul(dst[:, :, SLOT0[c]:SLOT0[c] + SLOTS[c]],
                                                    pairs[:, half, g % HALF, START[c]:START[c] + ROWS],
                                                    diag[:, n, g, :, FIRST[c]:ONE + 1], start=True, stop=True)
                    last.then_inc(t_full, 1)

            def cin(t, n):
                eng.wait_ge(t_out, UNITS * t + UNITS)
                if isinstance(t, int) and t == 0:
                    eng.wait_ge(prep_out, PREPS)
                else:
                    eng.wait_ge(z_out, t)
                for c in range(3):
                    s = SLOT0[c] + SLOTS[c] - 1
                    nc.tensor.matmul(z_ps[:, 0:NP], v[0:WIDTH[c], s, :], tsum[0:WIDTH[c], n, s, :],
                                     start=(c == 0), stop=(c == 2))
                nc.tensor.matmul(z_ps[:, NP:2 * NP], b2row[0:1, :], tsum[0:1, n, SLOT0[0] + ONE, :],
                                 start=True, stop=False)
                for c in range(3):
                    for s in range(SLOT0[c], SLOT0[c] + SLOTS[c] - 1):
                        last = nc.tensor.matmul(z_ps[:, NP:2 * NP], v[0:WIDTH[c], s, :], tsum[0:WIDTH[c], n, s, :],
                                                start=False, stop=(s == NSLOT - 2))
                last.then_inc(z_full, 1)

            def layer1(t):
                eng.wait_ge(z_out, t + 1)
                if not (isinstance(t, int) and t < 1):
                    eng.wait_ge(h1_out, t)
                for a in range(N1 // NP):
                    dst = h1_ps[:, a * NP:(a + 1) * NP]
                    cols = slice(a * NP, (a + 1) * NP)
                    for s in range(2):
                        nc.tensor.matmul(dst, top1[:, s, cols], z[:, s, :], start=(s == 0), stop=False)
                    last = nc.tensor.matmul(dst, top1d[0:ND + 1, cols], denseT[0:ND + 1, bass.ts(t, NP)],
                                            start=False, stop=True)
                last.then_inc(h1_full, 1)

            def layer2(t):
                eng.wait_ge(h1_out, t + 1)
                if not (isinstance(t, int) and t < 1):
                    eng.wait_ge(h2_out, t)
                for a in range(N2 // NP):
                    for s in range(N1 // NP):
                        last = nc.tensor.matmul(h2_ps[:, a * NP:(a + 1) * NP], top2[:, s, a:N2:N2 // NP],
                                                h1[:, s, :], start=(s == 0), stop=(s == N1 // NP - 1))
                last.then_inc(h2_full, 1)

            def layer3(t):
                eng.wait_ge(h2_out, t + 1)
                if not (isinstance(t, int) and t < 1):
                    eng.wait_ge(y_out, t)
                for s in range(N2 // NP):
                    last = nc.tensor.matmul(y_ps[0:1, 0:NP], top3[:, s:s + 1], h2[:, s, :],
                                            start=(s == 0), stop=(s == N2 // NP - 1))
                last.then_inc(y_full, 1)

            def step(t, n):
                known = isinstance(t, int)
                if not known or t < TILES:
                    t_units(t, n, 0)
                if not known or t >= 2:
                    layer1(t - 2)
                if not known or t < TILES:
                    t_units(t, n, 1)
                if not known or t >= 2:
                    layer2(t - 2)
                if not known or 1 <= t <= TILES:
                    cin(t - 1, 1 - n)
                if not known or t >= 2:
                    layer3(t - 2)

            eng.wait_ge(consts_ready, 1)
            eng.wait_ge(top_in, 16 * LOADS_TOP)
            for t in range(4):
                step(t, t % 2)
            with eng.Fori(2, TILES // 2) as i:
                for n in range(2):
                    step(2 * i + n, n)
            for t in range(TILES, TILES + 2):
                step(t, t % 2)


def kernel(**inputs):
    import numpy as np
    import concourse.bacc as bacc
    from concourse.bass_utils import run_bass_kernel_spmd

    nc = bacc.Bacc("TRN2", target_bir_lowering=False, num_devices=1)
    arrays = {}

    def dram(name):
        a = np.ascontiguousarray(inputs[name])
        arrays[f"in_{name}"] = a
        return nc.dram_tensor(f"in_{name}", a.shape, mybir.dt.from_np(a.dtype), kind="ExternalInput").ap()

    out = nc.dram_tensor("out_y", (B, 1), fp32, kind="ExternalOutput").ap()
    build(nc, dram("dense_ctx"), dram("ids"), [dram(f"tbl_{f}") for f in range(F)],
          dram("W_top1"), dram("b_top1"), dram("W_top2"), dram("b_top2"), dram("W_top3"),
          dram("L0_rec_W1"), dram("L0_rec_b1"), dram("L0_rec_W2"), dram("L0_rec_b2"), out)
    r = run_bass_kernel_spmd(nc, [arrays], core_ids=[0])
    return r.results[0]["out_y"]
```

```python
from contextlib import ExitStack

import concourse.bass as bass
from concourse import mybir

fp32 = mybir.dt.float32
int32 = mybir.dt.int32
ALU = mybir.AluOpType
ACT = mybir.ActivationFunctionType

NP = 128
B, F, K = 2048, 26, 32
H = 128
ND = 16
N1, N2 = 512, 256
TILES = B // NP
Q = NP // K
GROUPS = NP // Q
HALF = GROUPS // 2
UNIT = 4
UNITS = GROUPS // UNIT
BANK = 512

HF = F // 2


def tri(r):
    return r * (r + 1) // 2


NPAIR = tri(HF)
CONST = NPAIR
FIELD0 = 96
ROWS = FIELD0 + HF
ONE = F
TS = F + 1

PACK4 = [(0, 4), (4, 7)]
PACK2 = (7, 10)
PLAIN = (10, HF)
CROSS = [(0, 4), (4, 7), (7, 10), (10, 13)]

P4, P2, PX = 0, 4, 7
NPACK = PX + 4
V_ONE = 0
V_CROSS = 2
V_OTHER = V_CROSS + 4
V_PLAIN = V_OTHER + F
V_P4 = V_PLAIN + 2 * (HF - PLAIN[0])
V_P2 = V_P4 + 4
NV = V_P2 + 3
K4, K2, KX = 96 + tri(7), 64 + tri(10), 96 + HF


def build(nc, dense_ctx, ids, tables, W_top1, b_top1, W_top2, b_top2, W_top3, W1, b1, W2, b2, out):
    ctx = ExitStack()
    with ctx:
        def sb(name, shape, dt=fp32):
            return ctx.enter_context(nc.sbuf_tensor(name, shape, dt))

        def sem(name):
            return ctx.enter_context(nc.semaphore(name))

        idx = [sb(f"idx{n}", [NP, F], int32) for n in range(2)]
        emb = [sb(f"emb{n}", [NP, F * K]) for n in range(2)]
        embT = [sb(f"embT{n}", [NP, F * GROUPS]) for n in range(2)]
        diag = sb("diag", [NP, 2, GROUPS, Q, F + 1])
        PAIRS_SIZE, PACK_SIZE = 2 * HALF * 2 * ROWS, 2 * NPACK * NP
        work = sb("work", [NP, PAIRS_SIZE + PACK_SIZE])
        pairs = work[:, 0:PAIRS_SIZE].rearrange("p (n g c x) -> p n g c x", n=2, g=HALF, c=2)
        packs = work[:, PAIRS_SIZE:PAIRS_SIZE + PACK_SIZE].rearrange("p (n s b) -> p n s b", n=2, s=NPACK)
        t_area = sb("t_area", [NP, 2 * 2 * TS * NP])
        tsum = t_area[:, :].rearrange("p (n s b) -> p n s b", n=2, s=2 * TS)
        v = sb("v", [NP, NV, H])
        ident = sb("ident", [NP, NP])
        top1 = sb("top1", [NP, 2, N1])
        top1d = sb("top1d", [K, N1])
        top2 = sb("top2", [NP, N1 // NP, N2])
        top3 = sb("top3", [NP, N2 // NP])
        bias2 = sb("bias2", [NP, N2 // NP])
        b2k = sb("b2k", [NP, 1])
        denseT = sb("denseT", [K, B])
        z = sb("z", [NP, 2, NP])
        h1 = sb("h1", [NP, N1 // NP, NP])
        h2 = sb("h2", [NP, N2 // NP, NP])
        y = sb("y", [1, B])

        moved = work[:, 0:F * F * HF].rearrange("p (c x y z) -> p c x y z", c=2, x=HF, y=F)
        assert F * F * HF <= PAIRS_SIZE + PACK_SIZE
        cut = [0]

        def part_of_t_area(size):
            cut[0] += size
            assert cut[0] <= 2 * 2 * TS * NP
            return t_area[:, cut[0] - size:cut[0]]

        w2raw = part_of_t_area(H * F).rearrange("p (i m) -> p i m", m=F)
        w2T = part_of_t_area(F * H).rearrange("p (m h) -> p m h", h=H)
        extra = part_of_t_area(2 * F * NPAIR).rearrange("p (c y x) -> p c y x", c=2, y=F)
        w1raw = part_of_t_area(F * F).rearrange("p (r c) -> p r c", c=F)
        w1p = part_of_t_area(2 * (NPAIR + 1)).rearrange("p (c x) -> p c x", c=2)
        w1s = part_of_t_area(2 * F * HF).rearrange("p (c y z) -> p c y z", c=2, y=F)
        dense, dense_q = (v[:, s:s + TILES * K // H, :].rearrange("p s (t c) -> p (s t) c", c=K) for s in (0, 4))

        psum = ctx.enter_context(nc.psum_tensor("psum", [NP, 8, BANK], fp32))
        z_ps, h1_ps, h2_ps, y_ps = (psum[:, n, :] for n in range(4, 8))

        w1_in, w2_in, b1_in, b2_in = sem("w1_in"), sem("w2_in"), sem("b1_in"), sem("b2_in")
        dense_in, top_in = sem("dense_in"), sem("top_in")
        idx_in = [sem(f"idx_in{n}") for n in range(2)]
        gathered = [sem(f"gathered{n}") for n in range(2)]
        ident_zero, ident_ready = sem("ident_zero"), sem("ident_ready")
        dense_pad = sem("dense_pad")
        dve_own = sem("dve_own")
        sym_ready = sem("sym_ready")
        prep_full = sem("prep_full")
        prep_out = sem("prep_out")
        extra_ready = sem("extra_ready")
        consts_ready = sem("consts_ready")
        embT_ready, diag_ready = sem("embT_ready"), sem("diag_ready")
        pairs_ready = sem("pairs_ready")
        packs_ready = sem("packs_ready")
        t_full, t_out = sem("t_full"), sem("t_out")
        z_full, z_out = sem("z_full"), sem("z_out")
        h1_full, h1_out = sem("h1_full"), sem("h1_out")
        h2_full, h2_out = sem("h2_full"), sem("h2_out")
        y_full, y_out = sem("y_full"), sem("y_out")
        stored = sem("stored")

        ROWS_IN = 16 * F

        w2T_jobs = [range(m, min(m + 4, F)) for m in range(0, F, 4)]
        v_jobs = []
        for c in range(2):
            for nu in range(0, HF, 4):
                v_jobs.append([("other", c, a, V_OTHER + c * HF + a, CONST + 1, 0) for a in range(nu, min(nu + 4, HF))])
        for c in range(2):
            own = []
            for j, (lo, hi) in enumerate(PACK4):
                own += [("own", c, mu, V_P4 + mu - lo, tri(mu + 1), 32 * (2 * c + j)) for mu in range(lo, hi)]
            own += [("own", c, mu, V_P2 + mu - PACK2[0], tri(mu + 1), 64 * c) for mu in range(*PACK2)]
            own += [("own", c, mu, V_PLAIN + c * (HF - PLAIN[0]) + mu - PLAIN[0], tri(mu + 1), 0) for mu in range(*PLAIN)]
            v_jobs += [own[n:n + 4] for n in range(0, len(own), 4)]
        for j, (lo, hi) in enumerate(CROSS):
            v_jobs.append([("cross", 0, nu, V_CROSS + nu - lo, HF, 32 * j) for nu in range(lo, hi)])
        v_jobs.append([("one", c, 0, V_ONE + c, NPAIR + 1 - c, 0) for c in range(2)])
        AFTER_W2T = len(w2T_jobs)
        AFTER_MOVED = AFTER_W2T + F
        PREPS = AFTER_MOVED + len(v_jobs)

        def prep_bank(n):
            return psum[:, 4 + n % 4, :]

        block = ctx.enter_context(nc.Block())

        @block.sync
        def _(eng):
            def load_idx(t, n):
                eng.dma_start(idx[n][:, :], ids[bass.ts(t, NP), :]).then_inc(idx_in[n], 16)

            load_idx(0, 0)
            load_idx(1, 1)
            eng.dma_start(w2raw.rearrange("p i m -> p (i m)"), W2.rearrange("h i m -> h (i m)")).then_inc(w2_in, 16)
            eng.dma_start(w1raw.rearrange("p r c -> p (r c)"), W1.rearrange("h r c -> h (r c)")).then_inc(w1_in, 16)
            for c in range(2):
                eng.dma_start(w1p[:, c, NPAIR:NPAIR + 1], b1.rearrange("(h o) -> h o", o=1)).then_inc(b1_in, 16)
            eng.dma_start(b2k[:, :], b2.rearrange("(h o) -> h o", o=1)).then_inc(b2_in, 16)
            eng.wait_ge(dense_pad, 1)
            eng.dma_start(dense[:, :, 0:ND], dense_ctx.rearrange("(t p) c -> p t c", p=NP)).then_inc(dense_in, 16)
            eng.dma_start(top1[:, :, :], W_top1[0:2 * H, :].rearrange("(a p) n -> p a n", p=NP)).then_inc(top_in, 16)
            eng.dma_start(top1d[0:ND, :], W_top1[2 * H:2 * H + ND, :]).then_inc(top_in, 16)
            eng.dma_start(top1d[ND:ND + 1, :], b_top1.rearrange("(o n) -> o n", o=1)).then_inc(top_in, 16)
            eng.dma_start(top2[:, :, :], W_top2.rearrange("(a p) n -> p a n", p=NP)).then_inc(top_in, 16)
            eng.dma_start(top3[:, :], W_top3.rearrange("(p a) o -> p (a o)", p=NP)).then_inc(top_in, 16)
            eng.dma_start(bias2[:, :], b_top2.rearrange("(p a) -> p a", p=NP)).then_inc(top_in, 16)
            with eng.Fori(1, TILES // 2) as i:
                for n in range(2):
                    eng.wait_ge(gathered[n], ROWS_IN * i)
                    load_idx(2 * i + n, n)
            eng.wait_ge(y_out, TILES)
            eng.dma_start(out.rearrange("b o -> o b"), y[:, :]).then_inc(stored, 16)
            eng.wait_ge(stored, 16)

        LOADS_TOP = 6

        @block.gpsimd
        def _(eng):
            eng.memset(ident[:, :], 0.0).then_inc(ident_zero, 1)
            eng.wait_ge(ident_zero, 1)
            eng.affine_select(out=ident[:, :], in_=ident[:, :], compare_op=ALU.not_equal, fill=1.0, base=0,
                              pattern=[[-1, NP]], channel_multiplier=1).then_inc(ident_ready, 1)

            def gather(i, n):
                eng.wait_ge(idx_in[n], 16 * i + 16)
                eng.nop(nofuse=True)
                for f in range(F):
                    eng.indirect_dma_start(
                        emb[n][:, f * K:(f + 1) * K], None, tables[f],
                        bass.IndirectOffsetOnAxis(ap=idx[n][:, f:f + 1], axis=0),
                    ).then_inc(gathered[n], 16)

            gather(0, 0)
            gather(0, 1)
            with eng.Fori(1, TILES // 2) as i:
                for n in range(2):
                    eng.wait_ge(embT_ready, 2 * i + n - 1)
                    gather(i, n)

        @block.vector
        def _(eng):
            own = 0

            nc.vector.memset(dense, 1.0).then_inc(dense_pad, 1)
            nc.vector.memset(extra, 0.0)
            nc.vector.memset(diag[:, :, :, :, :], 0.0).then_inc(dve_own, 1)
            own += 1
            eng.wait_ge(dve_own, own)
            for q in range(Q):
                part = slice(K * q, K * q + K)
                nc.vector.memset(diag[part, :, :, q, ONE], 1.0)

            eng.wait_ge(w1_in, 16)
            diagonal = w1raw.rearrange("p r c -> p (r c)")[:, 0:F * F:F + 1]
            nc.vector.tensor_scalar(diagonal, diagonal, 0.5, None, ALU.mult).then_inc(dve_own, 1)
            own += 1
            eng.wait_ge(dve_own, own)
            w1t = w1raw.rearrange("p r c -> p c r")
            for c in range(2):
                mine = slice(HF * c, HF * c + HF)
                for o in range(2):
                    rows = slice(HF * (c ^ o), HF * (c ^ o) + HF)
                    nc.vector.tensor_tensor(w1s[:, c, HF * o:HF * o + HF, :], w1raw[:, rows, mine],
                                            w1t[:, rows, mine], ALU.add)
                for r in range(HF):
                    rows, cols = HF * c + r, slice(HF * c, HF * c + r + 1)
                    last = nc.vector.tensor_tensor(w1p[:, c, tri(r):tri(r) + r + 1], w1raw[:, rows, cols],
                                                   w1t[:, rows, cols], ALU.add)
            last.then_inc(sym_ready, 1)

            eng.wait_ge(dense_in, 16)
            nc.vector.transpose(dense_q.rearrange("p t c -> p (t c)"), dense.rearrange("p t c -> p (t c)"))\
                .then_inc(dve_own, 1)
            own += 1
            eng.wait_ge(dve_own, own)
            for q in range(Q):
                dst = denseT[0:ND + 1, :].rearrange("p (t q g) -> p q t g", q=Q, g=GROUPS)[:, q]
                last = nc.vector.tensor_copy(dst, dense_q[K * q:K * q + ND + 1, :, :])
            last.then_inc(dve_own, 1)
            own += 1
            eng.wait_ge(dve_own, own)
            nc.vector.memset(v[:, :, :], 0.0)
            eng.wait_ge(b2_in, 16)
            nc.vector.tensor_scalar(b2k[:, :], b2k[:, :], float(K), None, ALU.mult).then_inc(consts_ready, 1)

            eng.wait_ge(prep_out, AFTER_MOVED)
            for c in range(2):
                m = moved[:, c]
                halves = bass.AP(m.tensor, m.offset, [list(m.ap[0]), [F * HF + 1, HF], [HF, F]])
                last = nc.vector.tensor_scalar(halves, halves, 0.5, None, ALU.mult)
            last.then_inc(dve_own, 1)
            own += 1
            eng.wait_ge(dve_own, own)
            for c in range(2):
                by_x = moved[:, c].rearrange("p x y z -> p y z x")
                for r in range(HF):
                    at = tri(r)
                    last = nc.vector.tensor_tensor(extra[:, c, r + 1:F, at:at + r + 1], moved[:, c, r, r + 1:F, 0:r + 1],
                                                   by_x[:, r + 1:F, r, 0:r + 1], ALU.add)
                    if r:
                        last = nc.vector.tensor_copy(extra[:, c, r, at:at + r], by_x[:, r, r, 0:r])
            last.then_inc(extra_ready, 1)

            eng.wait_ge(extra_ready, 1)
            nc.vector.memset(pairs[:, :, :, 0, CONST:FIELD0], 1.0)
            nc.vector.memset(pairs[:, :, :, 1, CONST:ROWS], 1.0)
            nc.vector.memset(packs, 0.0).then_inc(dve_own, 1)
            own += 1
            eng.wait_ge(dve_own, own)

            def tile(t, i, n):
                eng.wait_ge(gathered[n], ROWS_IN * i + ROWS_IN)
                if not (isinstance(t, int) and t < 2):
                    eng.wait_ge(diag_ready, t - 1)
                nc.vector.transpose(embT[n][:, :], emb[n][:, :]).then_inc(embT_ready, 1)
                eng.wait_ge(embT_ready, t + 1)
                e = embT[n][:, :].rearrange("p (m g) -> p g m", g=GROUPS)
                for half in range(2):
                    if not (isinstance(t, int) and t < 1):
                        eng.wait_ge(t_full, UNITS * t - UNITS + (UNITS // 2) * (half + 1))
                    g = slice(HALF * half, HALF * half + HALF)
                    for c in range(2):
                        for r in range(HF):
                            f = HF * c + r
                            nc.vector.tensor_tensor(pairs[:, half, :, c, tri(r):tri(r) + r + 1], e[:, g, HF * c:f + 1],
                                                    e[:, g, f:f + 1].broadcast_to([NP, HALF, r + 1]), ALU.mult)
                    nc.vector.tensor_copy(pairs[:, half, :, 0, FIELD0:ROWS], e[:, g, 0:HF]).then_inc(pairs_ready, 1)
                if not (isinstance(t, int) and t < 2):
                    eng.wait_ge(z_full, t - 1)
                eng.wait_ge(t_out, UNITS * t + UNITS)
                for c in range(2):
                    s = c * TS + c * HF
                    for j, (lo, hi) in enumerate(PACK4):
                        at = 32 * (2 * c + j)
                        nc.vector.tensor_copy(packs[at:at + tri(hi), n, P4:P4 + hi - lo, :],
                                              tsum[0:tri(hi), n, s + lo:s + hi, :])
                    lo, hi = PACK2
                    nc.vector.tensor_copy(packs[64 * c:64 * c + tri(hi), n, P2:P2 + hi - lo, :],
                                          tsum[0:tri(hi), n, s + lo:s + hi, :])
                for j, (lo, hi) in enumerate(CROSS):
                    last = nc.vector.tensor_copy(packs[32 * j:32 * j + HF, n, PX:PX + hi - lo, :],
                                                 tsum[FIELD0:ROWS, n, HF + lo:HF + hi, :])
                last.then_inc(packs_ready, 1)

            tile(0, 0, 0)
            tile(1, 0, 1)
            with eng.Fori(1, TILES // 2) as i:
                for n in range(2):
                    tile(2 * i + n, i, n)

        @block.scalar
        def _(eng):
            for n, ms in enumerate(w2T_jobs):
                eng.wait_ge(prep_full, n + 1)
                nc.scalar.copy(w2T[:, ms[0]:ms[-1] + 1, :].rearrange("p m h -> p (m h)"),
                               prep_bank(n)[:, 0:len(ms) * H]).then_inc(prep_out, 1)
            for x in range(F):
                n = AFTER_W2T + x
                eng.wait_ge(prep_full, n + 1)
                nc.scalar.copy(moved[:, x // HF, x % HF].rearrange("p y z -> p (y z)"), prep_bank(n)[:, 0:F * HF])\
                    .then_inc(prep_out, 1)
            eng.wait_ge(consts_ready, 1)
            for n, job in enumerate(v_jobs, AFTER_MOVED):
                eng.wait_ge(prep_full, n + 1)
                if job[0][0] == "own" or job[0][0] == "one":
                    for a, (_, _, _, s, rows, at) in enumerate(job):
                        last = nc.scalar.copy(v[at:at + rows, s, :], prep_bank(n)[0:rows, a * H:(a + 1) * H])
                else:
                    _, _, _, s, rows, at = job[0]
                    last = nc.scalar.copy(v[at:at + rows, s:s + len(job), :].rearrange("p s h -> p (s h)"),
                                          prep_bank(n)[0:rows, 0:len(job) * H])
                last.then_inc(prep_out, 1)

            def fill_diag(t, n):
                eng.wait_ge(embT_ready, t + 1)
                if not (isinstance(t, int) and t < 2):
                    eng.wait_ge(t_full, UNITS * t - UNITS)
                for q in range(Q):
                    part = slice(K * q, K * q + K)
                    last = nc.scalar.copy(diag[part, n, :, q, 0:F],
                                          embT[n][part, :].rearrange("p (m g) -> p g m", g=GROUPS))
                last.then_inc(diag_ready, 1)

            def unit_out(t, n, u):
                if u == 0 and not (isinstance(t, int) and t < 2):
                    eng.wait_ge(z_full, t - 1)
                    eng.wait_ge(packs_ready, t - 1)
                eng.wait_ge(t_full, UNITS * t + u + 1)
                src = psum[0:ROWS, 2 * (u % 2):2 * (u % 2) + 2, :].rearrange("p a (b c) -> p (a b) c", b=2)
                src = src[:, :, 0:Q * 2 * TS].rearrange("p g (q s) -> p g q s", q=Q)
                dst = tsum[0:ROWS, n].rearrange("p s (q g) -> p g q s", q=Q)[:, UNIT * u:UNIT * u + UNIT]
                nc.scalar.copy(dst, src).then_inc(t_out, 1)

            def z_move(t):
                if not (isinstance(t, int) and t < 1):
                    eng.wait_ge(h1_full, t)
                eng.wait_ge(z_full, t + 1)
                nc.scalar.copy(z[:, 0, :], z_ps[:, 0:NP])
                nc.scalar.activation(z[:, 1, :], z_ps[:, NP:2 * NP], ACT.Identity, bias=b2k[:, 0:1]).then_inc(z_out, 1)

            def h1_move(t):
                if not (isinstance(t, int) and t < 1):
                    eng.wait_ge(h2_full, t)
                eng.wait_ge(h1_full, t + 1)
                nc.scalar.activation(h1[:, :, :].rearrange("p a b -> p (a b)"), h1_ps, ACT.Relu).then_inc(h1_out, 1)

            def h2_move(t):
                if not (isinstance(t, int) and t < 1):
                    eng.wait_ge(y_full, t)
                eng.wait_ge(h2_full, t + 1)
                for a in range(N2 // NP):
                    last = nc.scalar.activation(h2[:, a, :], h2_ps[:, a * NP:(a + 1) * NP], ACT.Relu,
                                                bias=bias2[:, a:a + 1])
                last.then_inc(h2_out, 1)

            def y_move(t):
                eng.wait_ge(y_full, t + 1)
                nc.scalar.copy(y[0:1, bass.ts(t, NP)], y_ps[0:1, 0:NP]).then_inc(y_out, 1)

            def step(t, n):
                known = isinstance(t, int)
                if not known or t < TILES:
                    for u in range(UNITS // 2):
                        unit_out(t, n, u)
                if not known or t >= 2:
                    h1_move(t - 2)
                if not known or t < TILES:
                    for u in range(UNITS // 2, UNITS):
                        unit_out(t, n, u)
                if not known or t >= 2:
                    h2_move(t - 2)
                if not known or t + 1 < TILES:
                    fill_diag(t + 1, 1 - n)
                if not known or 1 <= t <= TILES:
                    z_move(t - 1)
                if not known or t >= 2:
                    y_move(t - 2)

            eng.wait_ge(top_in, 16 * LOADS_TOP)
            fill_diag(0, 0)
            for t in range(4):
                step(t, t % 2)
            with eng.Fori(2, TILES // 2 - 1) as i:
                for n in range(2):
                    step(2 * i + n, n)
            for t in range(TILES - 2, TILES + 2):
                step(t, t % 2)

        @block.tensor
        def _(eng):
            def free_bank(n):
                if n >= 4:
                    eng.wait_ge(prep_out, n - 3)

            eng.wait_ge(ident_ready, 1)
            eng.wait_ge(w2_in, 16)
            for n, ms in enumerate(w2T_jobs):
                free_bank(n)
                for a, m in enumerate(ms):
                    last = nc.tensor.transpose(prep_bank(n)[:, a * H:(a + 1) * H], w2raw[:, :, m], ident[:, :])
                last.then_inc(prep_full, 1)
            eng.wait_ge(sym_ready, 1)
            for x in range(F):
                n = AFTER_W2T + x
                eng.wait_ge(prep_out, max(n - 3, x // 4 + 1))
                nc.tensor.matmul(prep_bank(n)[:, 0:F * HF], w2T[:, x, :],
                                 w1s[:, x // HF].rearrange("p y z -> p (y z)"),
                                 start=True, stop=True).then_inc(prep_full, 1)
            eng.wait_ge(b1_in, 32)
            eng.wait_ge(extra_ready, 1)
            for n, job in enumerate(v_jobs, AFTER_MOVED):
                free_bank(n)
                for a, (what, c, third, _, rows, _) in enumerate(job):
                    dst = prep_bank(n)[0:rows, a * H:(a + 1) * H]
                    if what == "one":
                        last = nc.tensor.matmul(dst, w1p[:, c, 0:rows], ident[:, :], start=True, stop=True)
                    elif what == "cross":
                        last = nc.tensor.matmul(dst, w1s[:, c, HF + third, 0:rows], ident[:, :], start=True, stop=True)
                    else:
                        y_local = third + HF * (what == "other")
                        m = HF * c + third if what == "own" else HF * (1 - c) + third
                        nc.tensor.matmul(dst, w1p[:, c, 0:rows], w2T[:, m, :], start=True, stop=False)
                        pr = min(rows, NPAIR)
                        last = nc.tensor.matmul(prep_bank(n)[0:pr, a * H:(a + 1) * H], extra[:, c, y_local, 0:pr],
                                                ident[:, :], start=False, stop=True)
                last.then_inc(prep_full, 1)

            def t_units(t, n, half):
                eng.wait_ge(pairs_ready, 2 * t + half + 1)
                if half == 0:
                    eng.wait_ge(diag_ready, t + 1)
                for u in range(half * UNITS // 2, (half + 1) * UNITS // 2):
                    if not (isinstance(t, int) and UNITS * t + u < 2):
                        eng.wait_ge(t_out, UNITS * t + u - 1)
                    for j in range(UNIT):
                        g = UNIT * u + j
                        at = (j % 2) * (BANK // 2)
                        dst = psum[0:ROWS, 2 * (u % 2) + j // 2, at:at + Q * 2 * TS]
                        dst = dst.rearrange("p (q s) -> p q s", q=Q)
                        for c in range(2):
                            last = nc.tensor.matmul(dst[:, :, c * TS:(c + 1) * TS], pairs[:, half, g % HALF, c, :],
                                                    diag[:, n, g, :, :], start=True, stop=True)
                    last.then_inc(t_full, 1)

            def cin(t, n):
                eng.wait_ge(packs_ready, t + 1)
                if isinstance(t, int) and t == 0:
                    eng.wait_ge(prep_out, PREPS)
                else:
                    eng.wait_ge(z_out, t)
                terms = [(V_ONE + c, tsum, c * TS + ONE, NPAIR + 1 - c) for c in range(2)]
                terms += [(V_CROSS + a, packs, PX + a, KX) for a in range(4)]
                for a, (s, src, slot, rows) in enumerate(terms):
                    nc.tensor.matmul(z_ps[:, 0:NP], v[0:rows, s, :], src[0:rows, n, slot, :],
                                     start=(a == 0), stop=(a == len(terms) - 1))
                terms = []
                for c in range(2):
                    terms += [(V_OTHER + c * HF + nu, tsum, c * TS + (1 - c) * HF + nu, CONST + 1) for nu in range(HF)]
                    terms += [(V_PLAIN + c * (HF - PLAIN[0]) + mu - PLAIN[0], tsum, c * TS + c * HF + mu, NPAIR)
                              for mu in range(*PLAIN)]
                terms += [(V_P4 + a, packs, P4 + a, K4) for a in range(4)]
                terms += [(V_P2 + a, packs, P2 + a, K2) for a in range(3)]
                for a, (s, src, slot, rows) in enumerate(terms):
                    last = nc.tensor.matmul(z_ps[:, NP:2 * NP], v[0:rows, s, :], src[0:rows, n, slot, :],
                                            start=(a == 0), stop=(a == len(terms) - 1))
                last.then_inc(z_full, 1)

            def layer1(t):
                eng.wait_ge(z_out, t + 1)
                if not (isinstance(t, int) and t < 1):
                    eng.wait_ge(h1_out, t)
                for a in range(N1 // NP):
                    dst = h1_ps[:, a * NP:(a + 1) * NP]
                    cols = slice(a * NP, (a + 1) * NP)
                    for s in range(2):
                        nc.tensor.matmul(dst, top1[:, s, cols], z[:, s, :], start=(s == 0), stop=False)
                    last = nc.tensor.matmul(dst, top1d[0:ND + 1, cols], denseT[0:ND + 1, bass.ts(t, NP)],
                                            start=False, stop=True)
                last.then_inc(h1_full, 1)

            def layer2(t):
                eng.wait_ge(h1_out, t + 1)
                if not (isinstance(t, int) and t < 1):
                    eng.wait_ge(h2_out, t)
                for a in range(N2 // NP):
                    for s in range(N1 // NP):
                        last = nc.tensor.matmul(h2_ps[:, a * NP:(a + 1) * NP], top2[:, s, a:N2:N2 // NP],
                                                h1[:, s, :], start=(s == 0), stop=(s == N1 // NP - 1))
                last.then_inc(h2_full, 1)

            def layer3(t):
                eng.wait_ge(h2_out, t + 1)
                if not (isinstance(t, int) and t < 1):
                    eng.wait_ge(y_out, t)
                for s in range(N2 // NP):
                    last = nc.tensor.matmul(y_ps[0:1, 0:NP], top3[:, s:s + 1], h2[:, s, :],
                                            start=(s == 0), stop=(s == N2 // NP - 1))
                last.then_inc(y_full, 1)

            def step(t, n):
                known = isinstance(t, int)
                if not known or t < TILES:
                    t_units(t, n, 0)
                if not known or t >= 2:
                    layer1(t - 2)
                if not known or t < TILES:
                    t_units(t, n, 1)
                if not known or t >= 2:
                    layer2(t - 2)
                if not known or 1 <= t <= TILES:
                    cin(t - 1, 1 - n)
                if not known or t >= 2:
                    layer3(t - 2)

            eng.wait_ge(consts_ready, 1)
            eng.wait_ge(top_in, 16 * LOADS_TOP)
            for t in range(4):
                step(t, t % 2)
            with eng.Fori(2, TILES // 2) as i:
                for n in range(2):
                    step(2 * i + n, n)
            for t in range(TILES, TILES + 2):
                step(t, t % 2)


def kernel(**inputs):
    import numpy as np
    import concourse.bacc as bacc
    from concourse.bass_utils import run_bass_kernel_spmd

    nc = bacc.Bacc("TRN2", target_bir_lowering=False, num_devices=1)
    arrays = {}

    def dram(name):
        a = np.ascontiguousarray(inputs[name])
        arrays[f"in_{name}"] = a
        return nc.dram_tensor(f"in_{name}", a.shape, mybir.dt.from_np(a.dtype), kind="ExternalInput").ap()

    out = nc.dram_tensor("out_y", (B, 1), fp32, kind="ExternalOutput").ap()
    build(nc, dram("dense_ctx"), dram("ids"), [dram(f"tbl_{f}") for f in range(F)],
          dram("W_top1"), dram("b_top1"), dram("W_top2"), dram("b_top2"), dram("W_top3"),
          dram("L0_rec_W1"), dram("L0_rec_b1"), dram("L0_rec_W2"), dram("L0_rec_b2"), out)
    r = run_bass_kernel_spmd(nc, [arrays], core_ids=[0])
    return r.results[0]["out_y"]
```

```python
from contextlib import ExitStack

import concourse.bass as bass
from concourse import mybir

fp32 = mybir.dt.float32
int32 = mybir.dt.int32
bf16 = mybir.dt.bfloat16
fp32r = mybir.dt.float32r
ALU = mybir.AluOpType
ACT = mybir.ActivationFunctionType

NP = 128
B, F, K = 2048, 26, 32
H = 128
ND = 16
N1, N2 = 512, 256
TILES = B // NP
Q = NP // K
GROUPS = NP // Q
HALF = GROUPS // 2
UNIT = 2
UNITS = GROUPS // UNIT
BANK = 512

HF = F // 2


def tri(r):
    return r * (r + 1) // 2


NPAIR = tri(HF)
CONST = NPAIR
FIELD0 = 96
ROWS = FIELD0 + HF
ONE = F
TS = F + 1

LOW = 64
UPPER = CONST + 1 - LOW
SMALL = 7
TALL = 10

P28, N28 = 0, HF - 1
NU_LAST, MU_SMALL, MU_TALL = 0, 1, 1 + SMALL
P1, N1S = P28 + N28, 4
CROSS = [(0, 4), (4, 7), (7, 10), (10, 13)]
ONE_UPPER = [(1, 3), (2, 3)]
NPACK = P1 + N1S
KP = 96 + UPPER

V_ONE, V_P1 = 0, 1
V_OTHER = V_P1 + N1S
V_OWN = V_OTHER + HF
V_P28 = V_OWN + HF - SMALL
NV = V_P28 + N28

PARTS = 3


SHORTS = 3


def short_fields(rows):
    return sorted(sorted(range(F), key=lambda f: rows[f])[:SHORTS])


def build(nc, dense_ctx, ids, short_ids, tables, W_top1, b_top1, W_top2, b_top2, W_top3, W1, b1, W2, b2, out):
    ctx = ExitStack()
    with ctx:
        def sb(name, shape, dt=fp32):
            return ctx.enter_context(nc.sbuf_tensor(name, shape, dt))

        def sem(name):
            return ctx.enter_context(nc.semaphore(name))

        SHORT = short_fields([table.shape[0] for table in tables])
        SHORT_ROWS = tables[SHORT[0]].shape[0]
        assert all(tables[f].shape[0] == SHORT_ROWS for f in SHORT)
        CHUNK = max(n for n in range(1, NP + 1) if SHORT_ROWS % n == 0)
        CHUNKS = SHORT_ROWS // CHUNK

        idx = [sb(f"idx{n}", [NP, F], int32) for n in range(2)]
        emb = [sb(f"emb{n}", [NP, F * K]) for n in range(2)]
        embT = [sb(f"embT{n}", [NP, F * GROUPS]) for n in range(2)]
        diag = sb("diag", [NP, GROUPS, Q, F + 1])
        PAIRS_SIZE, PACK_SIZE = 2 * HALF * 2 * ROWS, 2 * NPACK * NP
        work = sb("work", [NP, PAIRS_SIZE + PACK_SIZE])
        pairs = work[:, 0:PAIRS_SIZE].rearrange("p (n g c x) -> p n g c x", n=2, g=HALF, c=2)
        packs = work[:, PAIRS_SIZE:PAIRS_SIZE + PACK_SIZE].rearrange("p (n s b) -> p n s b", n=2, s=NPACK)
        t_area = sb("t_area", [NP, 2 * 2 * TS * NP])
        tsum = t_area[:, :].rearrange("p (n s b) -> p n s b", n=2, s=2 * TS)
        v = sb("v", [NP, NV, H])
        ident = sb("ident", [NP, NP])
        top1_hi, top1_lo = (sb(f"top1_{part}", [NP, 2, N1], fp32r) for part in ("hi", "lo"))
        top1d = sb("top1d", [3 * K, N1 + N2], fp32r)
        top2_hi, top2_lo = (sb(f"top2_{part}", [NP, N1 // NP, N2], fp32r) for part in ("hi", "lo"))
        top3 = sb("top3", [NP, N2])
        b2k = sb("b2k", [NP, 1])
        denseT = sb("denseT", [3 * K, B], fp32r)
        z_hi, z_lo = (sb(f"z_{part}", [NP, 2, 2, NP], fp32r) for part in ("hi", "lo"))
        h1_hi, h1_lo = (sb(f"h1_{part}", [NP, 2, N1], fp32r) for part in ("hi", "lo"))
        y = sb("y", [NP, TILES])
        yT = sb("yT", [TILES, NP])[:, :]
        zero = sb("zero", [NP, 1])
        table_parts = sb("table_parts", [CHUNK, SHORTS, CHUNKS, PARTS, K], bf16)
        ids_all = sb("ids_all", [CHUNK, SHORTS, NP], int32)
        ids_left = sb("ids_left", [CHUNK, SHORTS, NP], bf16)
        onehot = sb("onehot", [CHUNK, CHUNKS, SHORTS, NP], bf16)
        first_row_int, first_row = sb("first_row_int", [NP, 1], int32), sb("first_row", [NP, 1])

        moved = work[:, 0:F * F * HF].rearrange("p (c x y z) -> p c x y z", c=2, x=HF, y=F)
        assert F * F * HF <= PAIRS_SIZE + PACK_SIZE
        T_SIZE = 2 * TS * NP
        cut = [0, 0]

        def part_of_tsum(n, size):
            cut[n] += size
            assert cut[n] <= T_SIZE
            return t_area[:, n * T_SIZE + cut[n] - size:n * T_SIZE + cut[n]]

        w2raw = part_of_tsum(0, H * F).rearrange("p (i m) -> p i m", m=F)
        w1raw = part_of_tsum(0, F * F).rearrange("p (r c) -> p r c", c=F)
        w2T = part_of_tsum(1, F * H).rearrange("p (m h) -> p m h", h=H)
        w1p = part_of_tsum(1, 2 * (NPAIR + 1)).rearrange("p (c x) -> p c x", c=2)
        w1s = [part_of_tsum(1, F * HF).rearrange("p (y z) -> p y z", y=F) for c in range(2)]
        top1_raw = part_of_tsum(0, 2 * N1).rearrange("p (a n) -> p a n", a=2)
        extra0 = sb("extra0", [NP, F, NPAIR])
        raw_tables, raw_left = (part_of_tsum(0, SHORTS * CHUNKS * K)[0:CHUNK, :].rearrange("p (j c k) -> p j c k", j=SHORTS, c=CHUNKS)
                                for n in range(2))
        extra = [extra0[:, :, :], part_of_tsum(1, F * NPAIR).rearrange("p (y x) -> p y x", y=F)]
        dense, dense_hi, dense_lo = (v[:, s:s + TILES * K // H, :].rearrange("p s (t c) -> p (s t) c", c=K)
                                     for s in (0, 4, 8))
        top_raw = v[0:3 * K, 12:12 + (N1 + N2) // H, :].rearrange("p s h -> p (s h)")
        assert 12 + (N1 + N2) // H <= V_OWN
        assert F * F * HF <= PAIRS_SIZE + PACK_SIZE // 2
        top2_raw = packs[:, 1, 0:8, :].rearrange("p (a s) b -> p a (s b)", a=N1 // NP)
        dense_hiT, dense_loT = (packs[:, 1, s:s + TILES * K // NP, :].rearrange("p s (t c) -> p (s t) c", c=K)
                                for s in (8, 12))

        psum = ctx.enter_context(nc.psum_tensor("psum", [NP, 8, BANK], fp32))
        T_BANKS = 3
        z_ps, h2_ps, rows_ps = (psum[:, n, :] for n in (3, 6, 7))
        yT_ps = rows_ps
        h1_ps = psum[:, 4:6, :].rearrange("p c (a n b) -> p (c a) n b", n=2, b=NP)

        w1_in, w2_in, b1_in, b2_in = sem("w1_in"), sem("w2_in"), sem("b1_in"), sem("b2_in")
        dense_in, top_in = sem("dense_in"), sem("top_in")
        idx_in = [sem(f"idx_in{n}") for n in range(2)]
        gathered = [[sem(f"gathered{n}_{c}") for c in range(2)] for n in range(2)]
        short_in = sem("short_in")
        ids_in = sem("ids_in")
        rows_known = sem("rows_known")
        left_ready = sem("left_ready")
        onehot_ready = sem("onehot_ready")
        rows_full, rows_ready = sem("rows_full"), sem("rows_ready")
        ident_zero, ident_ready = sem("ident_zero"), sem("ident_ready")
        zero_ready, diag_zero = sem("zero_ready"), sem("diag_zero")
        v_zero, packs_zero = sem("v_zero"), sem("packs_zero")
        dense_pad = sem("dense_pad")
        dense_ready = sem("dense_ready")
        dve_own = sem("dve_own")
        sym_ready = sem("sym_ready")
        prep_full = sem("prep_full")
        prep_out = sem("prep_out")
        extra_ready = sem("extra_ready")
        consts_ready = sem("consts_ready")
        embT_ready, diag_ready = sem("embT_ready"), sem("diag_ready")
        pairs_ready = sem("pairs_ready")
        pieces_out, packs_ready = sem("pieces_out"), sem("packs_ready")
        t_full, t_out = sem("t_full"), sem("t_out")
        z_full, z_out = sem("z_full"), sem("z_out")
        h1_full, h1_out = sem("h1_full"), sem("h1_out")
        top1_in, top1_ready = sem("top1_in"), sem("top1_ready")
        top2_in, top2_ready = sem("top2_in"), sem("top2_ready")
        z_lo_ready, h1_lo_ready = sem("z_lo_ready"), sem("h1_lo_ready")
        h2_full, y_ready = sem("h2_full"), sem("y_ready")
        yT_full, yT_ready = sem("yT_full"), sem("yT_ready")
        stored = sem("stored")

        def rows_in(i, n, c):
            short = sum(f // HF == c for f in SHORT)
            return 16 * (HF - short) * (i + 1) + (16 * short if n == 0 else 0)

        w2T_jobs = [range(m, min(m + 4, F)) for m in range(0, F, 4)]
        v_jobs = [([("one", c, 0, CONST + 1 - c) for c in range(2)],
                   [(c, 1, 0, LOW, LOW * c, V_ONE) for c in range(2)]
                   + [(c, 1, LOW, CONST + 1 - c, 32 * ONE_UPPER[c][0], V_P1 + ONE_UPPER[c][1]) for c in range(2)])]
        for j, (lo, hi) in enumerate(CROSS):
            v_jobs.append(([("cross", 0, nu, HF) for nu in range(lo, hi)], [(0, hi - lo, 0, HF, 32 * j, V_P1)]))
        JOBS_W1 = len(v_jobs)
        for c in range(2):
            for lo in range(0, HF, 4):
                hi = min(lo + 4, HF)
                at = (32 * 2 * c, V_P28 + lo) if lo < N28 else (32 * (2 * c + 1), V_P28 + NU_LAST)
                v_jobs.append(([("other", c, nu, CONST + 1) for nu in range(lo, hi)],
                               [(0, hi - lo, 0, LOW, LOW * c, V_OTHER + lo), (0, hi - lo, LOW, CONST + 1, *at)]))
            for lo in range(0, HF, 4):
                moves = []
                for mu in range(lo, min(lo + 4, HF)):
                    rows = tri(mu + 1)
                    if mu < SMALL:
                        moves.append((mu - lo, 1, 0, rows, 32 * (2 * c + 1), V_P28 + MU_SMALL + mu))
                        continue
                    moves.append((mu - lo, 1, 0, min(rows, LOW), LOW * c, V_OWN + mu - SMALL))
                    if mu >= TALL:
                        moves.append((mu - lo, 1, LOW, rows, 32 * (2 * c + 1), V_P28 + MU_TALL + mu - TALL))
                v_jobs.append(([("own", c, mu, tri(mu + 1)) for mu in range(lo, min(lo + 4, HF))], moves))
        AFTER_W2T = len(w2T_jobs)
        AFTER_MOVED = AFTER_W2T + F
        AFTER_V0 = AFTER_MOVED + (JOBS_W1 + len(v_jobs)) // 2
        PREPS = AFTER_MOVED + len(v_jobs)

        def prep_bank(n):
            return psum[:, 4 + n % 4, :]

        block = ctx.enter_context(nc.Block())

        @block.sync
        def _(eng):
            def load_idx(t, n):
                eng.dma_start(idx[n][:, :], ids[bass.ts(t, NP), :]).then_inc(idx_in[n], 16)

            def load_ids_all(t):
                src = short_ids[:, bass.ts(t, NP)].rearrange("(o j) b -> o j b", o=1)
                eng.dma_start(ids_all[:, :, :], src.broadcast_to([CHUNK, SHORTS, NP])).then_inc(ids_in, 16)

            load_idx(0, 0)
            load_idx(1, 1)
            eng.dma_start(w1raw.rearrange("p r c -> p (r c)"), W1.rearrange("h r c -> h (r c)")).then_inc(w1_in, 16)
            eng.dma_start(w2raw.rearrange("p i m -> p (i m)"), W2.rearrange("h i m -> h (i m)")).then_inc(w2_in, 16)
            for j in range(SHORTS):
                eng.dma_start(raw_tables[:, j].rearrange("p c k -> p (c k)"),
                              tables[SHORT[j]].rearrange("(p c) k -> p (c k)", c=CHUNKS)).then_inc(short_in, 16)
            load_ids_all(1)
            for c in range(2):
                eng.dma_start(w1p[:, c, NPAIR:NPAIR + 1], b1.rearrange("(h o) -> h o", o=1)).then_inc(b1_in, 16)
            eng.dma_start(b2k[:, :], b2.rearrange("(h o) -> h o", o=1)).then_inc(b2_in, 16)
            eng.wait_ge(dense_pad, 1)
            eng.dma_start(dense[:, :, 0:ND], dense_ctx.rearrange("(t p) c -> p t c", p=NP)).then_inc(dense_in, 16)
            eng.dma_start(top1_raw, W_top1[0:2 * H, :].rearrange("(a p) n -> p a n", p=NP)).then_inc(top1_in, 16)
            for at in (0, K, 2 * K):
                eng.dma_start(top_raw[at:at + ND, 0:N1], W_top1[2 * H:2 * H + ND, :]).then_inc(top_in, 16)
                eng.dma_start(top_raw[at + ND:at + ND + 1, N1:N1 + N2], b_top2.rearrange("(o n) -> o n", o=1)).then_inc(top_in, 16)
                eng.dma_start(top_raw[at + ND:at + ND + 1, 0:N1], b_top1.rearrange("(o n) -> o n", o=1)).then_inc(top_in, 16)
            eng.dma_start(top3[:, :], W_top3.rearrange("n o -> o n").broadcast_to([NP, N2])).then_inc(top_in, 16)
            eng.dma_start(top2_raw, W_top2.rearrange("(a p) n -> p a n", p=NP)).then_inc(top2_in, 16)

            def next_ids(i, n):
                t = 2 * i + n
                eng.wait_ge(embT_ready, 2 * t - 2)
                load_idx(t, n)
                load_ids_all(t)

            with eng.Fori(1, TILES // 2) as i:
                for n in range(2):
                    next_ids(i, n)
            eng.wait_ge(yT_ready, 1)
            eng.dma_start(out.rearrange("(t p) o -> t (p o)", p=NP), yT).then_inc(stored, 16)
            eng.wait_ge(stored, 16)

        LOADS_TOP = 10

        @block.gpsimd
        def _(eng):
            eng.memset(ident[:, :], 0.0).then_inc(ident_zero, 1)
            eng.wait_ge(ident_zero, 1)
            eng.affine_select(out=ident[:, :], in_=ident[:, :], compare_op=ALU.not_equal, fill=1.0, base=0,
                              pattern=[[-1, NP]], channel_multiplier=1).then_inc(ident_ready, 1)

            eng.iota(first_row_int[:, :], pattern=[[0, 1]], base=0, channel_multiplier=CHUNKS).then_inc(rows_known, 1)

            def gather(i, n):
                eng.wait_ge(idx_in[n], 16 * i + 16)
                eng.nop(nofuse=True)
                for f in range(F):
                    if f in SHORT and not (isinstance(i, int) and 2 * i + n == 0):
                        continue
                    eng.indirect_dma_start(
                        emb[n][:, f * K:(f + 1) * K], None, tables[f],
                        bass.IndirectOffsetOnAxis(ap=idx[n][:, f:f + 1], axis=0),
                    ).then_inc(gathered[n][f // HF], 16)

            gather(0, 0)
            gather(0, 1)
            with eng.Fori(1, TILES // 2) as i:
                for n in range(2):
                    eng.wait_ge(embT_ready, 2 * (2 * i + n - 1))
                    gather(i, n)

        @block.vector
        def _(eng):
            own = 0

            nc.vector.memset(zero[:, :], 0.0).then_inc(zero_ready, 1)
            nc.vector.memset(top_raw[:, :], 0.0)
            nc.vector.memset(dense, 1.0).then_inc(dense_pad, 1)

            eng.wait_ge(w1_in, 16)
            diagonal = w1raw.rearrange("p r c -> p (r c)")[:, 0:F * F:F + 1]
            nc.vector.tensor_scalar(diagonal, diagonal, 0.5, None, ALU.mult).then_inc(dve_own, 1)
            own += 1
            eng.wait_ge(dve_own, own)
            w1t = w1raw.rearrange("p r c -> p c r")
            for c in range(2):
                mine = slice(HF * c, HF * c + HF)
                for o in range(2):
                    rows = slice(HF * (c ^ o), HF * (c ^ o) + HF)
                    nc.vector.tensor_tensor(w1s[c][:, HF * o:HF * o + HF, :], w1raw[:, rows, mine],
                                            w1t[:, rows, mine], ALU.add)
                for r in range(HF):
                    rows, cols = HF * c + r, slice(HF * c, HF * c + r + 1)
                    last = nc.vector.tensor_tensor(w1p[:, c, tri(r):tri(r) + r + 1], w1raw[:, rows, cols],
                                                   w1t[:, rows, cols], ALU.add)
            last.then_inc(sym_ready, 1)

            eng.wait_ge(diag_zero, 1)
            for q in range(Q):
                part = slice(K * q, K * q + K)
                nc.vector.memset(diag[part, :, q, ONE], 1.0)

            eng.wait_ge(dense_in, 16)
            nc.vector.tensor_copy(dense_hi.bitcast(fp32r), dense).then_inc(dve_own, 1)
            own += 1
            eng.wait_ge(dve_own, own)
            nc.vector.tensor_tensor(dense_lo, dense, dense_hi, ALU.subtract)
            nc.vector.transpose(dense_hiT.rearrange("p t c -> p (t c)"), dense_hi.rearrange("p t c -> p (t c)"))\
                .then_inc(dve_own, 1)
            own += 1
            eng.wait_ge(dve_own, own)
            nc.vector.transpose(dense_loT.rearrange("p t c -> p (t c)"), dense_lo.rearrange("p t c -> p (t c)"))\
                .then_inc(dve_own, 1)
            own += 1
            eng.wait_ge(dve_own, own)
            eng.wait_ge(top_in, 16 * LOADS_TOP)
            nc.vector.tensor_copy(top1d[:, :], top_raw[:, :]).then_inc(dve_own, 1)
            own += 1
            eng.wait_ge(dve_own, own)
            nc.vector.tensor_tensor(top1d[K:2 * K, :], top_raw[K:2 * K, :], top1d[K:2 * K, :].bitcast(fp32), ALU.subtract)
            nc.vector.memset(v[:, V_P1:V_P1 + N1S, :], 0.0)
            eng.wait_ge(b2_in, 16)
            nc.vector.tensor_scalar(b2k[:, :], b2k[:, :], float(K), None, ALU.mult).then_inc(consts_ready, 1)

            def make_onehot(t):
                eng.wait_ge(ids_in, 16 * t)
                nc.vector.tensor_scalar(ids_left[:, :, :], ids_all[:, :, :], first_row[0:CHUNK, 0:1], None,
                                        ALU.subtract).then_inc(left_ready, 1)
                eng.wait_ge(left_ready, t)
                for c in range(CHUNKS):
                    last = nc.vector.tensor_scalar(onehot[:, c], ids_left[:, :, :], float(c), None, ALU.is_equal)
                last.then_inc(onehot_ready, 1)

            def make_rows(t, n):
                eng.wait_ge(rows_full, t)
                for j, f in enumerate(SHORT):
                    last = nc.vector.tensor_reduce(
                        emb[n][:, f * K:f * K + K],
                        rows_ps[:, j * PARTS * K:(j + 1) * PARTS * K].rearrange("p (a k) -> p k a", a=PARTS),
                        mybir.AxisListType.X, ALU.add)
                last.then_inc(rows_ready, 1)

            eng.wait_ge(rows_known, 1)
            nc.vector.tensor_copy(first_row[:, :], first_row_int[:, :])
            eng.wait_ge(short_in, 16 * SHORTS)
            rest = raw_tables
            for part in range(PARTS):
                nc.vector.tensor_copy(table_parts[:, :, :, part, :], rest).then_inc(dve_own, 1)
                own += 1
                eng.wait_ge(dve_own, own)
                if part + 1 < PARTS:
                    nc.vector.tensor_tensor(raw_left, rest, table_parts[:, :, :, part, :], ALU.subtract).then_inc(dve_own, 1)
                    own += 1
                    eng.wait_ge(dve_own, own)
                    rest = raw_left

            for c in range(2):
                eng.wait_ge(prep_out, AFTER_W2T + HF * (c + 1))
                for x in range(HF):
                    halves = moved[:, c, x, x:F, x]
                    last = nc.vector.tensor_scalar(halves, halves, 0.5, None, ALU.mult)
                last.then_inc(dve_own, 1)
                own += 1
                eng.wait_ge(dve_own, own)
                by_x = moved[:, c].rearrange("p x y z -> p y z x")
                for r in range(HF):
                    at = tri(r)
                    nc.vector.memset(extra[c][:, r, at + r:at + r + 1], 0.0)
                    last = nc.vector.tensor_tensor(extra[c][:, r + 1:F, at:at + r + 1], moved[:, c, r, r + 1:F, 0:r + 1],
                                                   by_x[:, r + 1:F, r, 0:r + 1], ALU.add)
                    if r:
                        last = nc.vector.tensor_copy(extra[c][:, r, at:at + r], by_x[:, r, r, 0:r])
                last.then_inc(extra_ready, 1)

            eng.wait_ge(extra_ready, 2)
            nc.vector.memset(pairs[:, :, :, 0, CONST:FIELD0], 1.0)
            nc.vector.memset(pairs[:, :, :, 1, CONST:ROWS], 1.0)

            own_top1, own_top2, own_zeros = own + 1, own + 2, own + 3

            def split_top1():
                eng.wait_ge(top1_in, 16)
                nc.vector.tensor_copy(top1_hi[:, :, :], top1_raw).then_inc(dve_own, 1)
                eng.wait_ge(dve_own, own_top1)
                nc.vector.tensor_tensor(top1_lo[:, :, :], top1_raw, top1_hi[:, :, :].bitcast(fp32), ALU.subtract)\
                    .then_inc(top1_ready, 1)

            def split_top2():
                eng.wait_ge(top2_in, 16)
                nc.vector.tensor_copy(top2_hi[:, :, :], top2_raw).then_inc(dve_own, 1)
                eng.wait_ge(dve_own, own_top2)
                nc.vector.tensor_tensor(top2_lo[:, :, :], top2_raw, top2_hi[:, :, :].bitcast(fp32), ALU.subtract)\
                    .then_inc(top2_ready, 1)

            def zero_packs():
                nc.vector.memset(packs[:, 0, :, :], 0.0).then_inc(dve_own, 1)
                eng.wait_ge(dve_own, own_zeros)

            def lay_out_dense(at, src):
                dst = denseT[at:at + K, :].rearrange("p (t q g) -> p q t g", q=Q, g=GROUPS)
                for q in range(Q):
                    last = nc.vector.tensor_copy(dst[:, q], src[K * q:K * q + K, :, :])
                last.then_inc(dense_ready, 1)

            def pack(t, n):
                if not (isinstance(t, int) and t < 2):
                    eng.wait_ge(z_full, t - 1)
                eng.wait_ge(t_out, UNITS * t + UNITS)
                for c in range(2):
                    first, second = 32 * 2 * c, 32 * (2 * c + 1)
                    own_at, other_at = c * TS + c * HF, c * TS + (1 - c) * HF
                    upper = slice(LOW, LOW + UPPER)
                    nc.vector.tensor_copy(packs[first:first + UPPER, n, P28:P28 + N28, :],
                                          tsum[upper, n, other_at:other_at + N28, :])
                    nc.vector.tensor_copy(packs[second:second + UPPER, n, P28 + NU_LAST, :],
                                          tsum[upper, n, other_at + N28, :])
                    nc.vector.tensor_copy(packs[second:second + tri(SMALL), n, P28 + MU_SMALL:P28 + MU_SMALL + SMALL, :],
                                          tsum[0:tri(SMALL), n, own_at:own_at + SMALL, :])
                    nc.vector.tensor_copy(packs[second:second + UPPER, n, P28 + MU_TALL:P28 + MU_TALL + HF - TALL, :],
                                          tsum[upper, n, own_at + TALL:own_at + HF, :])
                    quadrant, slot = ONE_UPPER[c]
                    nc.vector.tensor_copy(packs[32 * quadrant:32 * quadrant + UPPER, n, P1 + slot, :],
                                          tsum[upper, n, c * TS + ONE, :])
                for j, (lo, hi) in enumerate(CROSS):
                    last = nc.vector.tensor_copy(packs[32 * j:32 * j + HF, n, P1:P1 + hi - lo, :],
                                                 tsum[FIELD0:ROWS, n, HF + lo:HF + hi, :])
                last.then_inc(pieces_out, 1)
                eng.wait_ge(pieces_out, t + 1)
                for dst, src, count in ((HF, TS, HF), (SMALL, TS + HF + SMALL, HF - SMALL), (ONE, TS + ONE, 1)):
                    last = nc.vector.tensor_copy(tsum[LOW:2 * LOW, n, dst:dst + count, :],
                                                 tsum[0:LOW, n, src:src + count, :])
                last.then_inc(packs_ready, 1)

            def z_low(t, n):
                eng.wait_ge(z_out, t + 1)
                nc.vector.tensor_tensor(z_lo[:, 0, n, :], z_ps[:, 0:NP], z_hi[:, 0, n, :].bitcast(fp32), ALU.subtract)
                nc.vector.scalar_tensor_tensor(z_lo[:, 1, n, :], z_ps[:, NP:2 * NP], b2k[:, 0:1],
                                               z_hi[:, 1, n, :].bitcast(fp32), ALU.add, ALU.subtract)\
                    .then_inc(z_lo_ready, 1)

            def h1_low(t, n):
                eng.wait_ge(h1_out, t + 1)
                nc.vector.scalar_tensor_tensor(h1_lo[:, n, :].rearrange("p (a b) -> p a b", b=NP), h1_ps[:, :, n, :], 0.0,
                                               h1_hi[:, n, :].bitcast(fp32).rearrange("p (a b) -> p a b", b=NP),
                                               ALU.max, ALU.subtract).then_inc(h1_lo_ready, 1)

            def make_y(t):
                eng.wait_ge(h2_full, t + 1)
                nc.vector.scalar_tensor_tensor(h2_ps[:, 0:N2], h2_ps[:, 0:N2], 0.0, top3[:, :], ALU.max, ALU.mult,
                                               accum_out=y[:, bass.ds(t, 1)]).then_inc(y_ready, 1)

            def tile(t, i, n):
                if not (isinstance(t, int) and t < 1):
                    eng.wait_ge(rows_ready, t)
                e = embT[n][:, :].rearrange("p (m g) -> p g m", g=GROUPS)
                for c in range(2):
                    eng.wait_ge(gathered[n][c], rows_in(i, n, c))
                    if c == 0 and not (isinstance(t, int) and t < 2):
                        eng.wait_ge(diag_ready, 2 * t - 2)
                    nc.vector.transpose(embT[n][:, c * HF * K:(c + 1) * HF * K], emb[n][:, c * HF * K:(c + 1) * HF * K])\
                        .then_inc(embT_ready, 1)
                eng.wait_ge(embT_ready, 2 * t + 2)
                for half in range(2):
                    if not (isinstance(t, int) and t < 1):
                        eng.wait_ge(t_full, UNITS * t - UNITS + (UNITS // 2) * (half + 1))
                    g = slice(HALF * half, HALF * half + HALF)
                    for c in range(2):
                        for r in range(HF):
                            f = HF * c + r
                            last = nc.vector.tensor_tensor(pairs[:, half, :, c, tri(r):tri(r) + r + 1], e[:, g, HF * c:f + 1],
                                                           e[:, g, f:f + 1].broadcast_to([NP, HALF, r + 1]), ALU.mult)
                        if c == 0:
                            nc.vector.tensor_copy(pairs[:, half, :, 0, FIELD0:ROWS], e[:, g, 0:HF])
                        else:
                            last.then_inc(pairs_ready, 1)
                known = isinstance(t, int)
                if known and t == 0:
                    split_top1()
                    split_top2()
                    zero_packs()
                    for at, src in ((0, dense_hiT), (K, dense_hiT), (2 * K, dense_loT)):
                        lay_out_dense(at, src)
                if not known or t >= 2:
                    z_low(t - 2, n)
                if not known or t >= 4:
                    make_y(t - 4)
                if not known or t >= 1:
                    pack(t - 1, 1 - n)
                if known and t == 1:
                    eng.wait_ge(packs_zero, 1)
                if not known or t >= 3:
                    h1_low(t - 3, 1 - n)
                if not isinstance(t, int) or t + 1 < TILES:
                    make_rows(t + 1, 1 - n)
                if not isinstance(t, int) or t + 2 < TILES:
                    make_onehot(t + 2)

            make_onehot(1)
            for t in range(4):
                tile(t, t // 2, t % 2)
            with eng.Fori(2, TILES // 2 - 1) as i:
                for n in range(2):
                    tile(2 * i + n, i, n)
            for t in range(TILES - 2, TILES):
                tile(t, t // 2, t % 2)
            pack(TILES - 1, 1)
            make_y(TILES - 4)
            h1_low(TILES - 3, 1)
            z_low(TILES - 2, 0)
            make_y(TILES - 3)
            z_low(TILES - 1, 1)
            for t in range(TILES - 2, TILES):
                h1_low(t, t % 2)
            for t in range(TILES - 2, TILES):
                make_y(t)
            eng.wait_ge(yT_full, 1)
            nc.vector.tensor_copy(yT, yT_ps[0:TILES, 0:NP]).then_inc(yT_ready, 1)

        @block.scalar
        def _(eng):
            eng.wait_ge(zero_ready, 1)
            nc.scalar.copy(diag[:, :, :, :].rearrange("p g q m -> p (g q m)"),
                           zero[:, :].broadcast_to([NP, GROUPS * Q * (F + 1)])).then_inc(diag_zero, 1)
            nc.scalar.copy(v[:, V_OWN:NV, :].rearrange("p s h -> p (s h)"), zero[:, :].broadcast_to([NP, (NV - V_OWN) * H]))\
                .then_inc(v_zero, 1)
            for n, ms in enumerate(w2T_jobs):
                eng.wait_ge(prep_full, n + 1)
                nc.scalar.copy(w2T[:, ms[0]:ms[-1] + 1, :].rearrange("p m h -> p (m h)"),
                               prep_bank(n)[:, 0:len(ms) * H]).then_inc(prep_out, 1)
            for x in range(F):
                n = AFTER_W2T + x
                eng.wait_ge(prep_full, n + 1)
                nc.scalar.copy(moved[:, x // HF, x % HF, x % HF:F, :].rearrange("p y z -> p (y z)"),
                               prep_bank(n)[:, 0:(F - x % HF) * HF]).then_inc(prep_out, 1)

            def v_out(lo, hi):
                for n in range(lo, hi):
                    eng.wait_ge(prep_full, n + 1)
                    for a, count, row, end, at, s in v_jobs[n - AFTER_MOVED][1]:
                        last = nc.scalar.copy(v[at:at + end - row, s:s + count, :],
                                              prep_bank(n)[row:end, a * H:(a + count) * H].rearrange("p (s h) -> p s h", h=H))
                    last.then_inc(prep_out, 1)

            def fill_diag(t, n, half, quadrants=range(Q)):
                eng.wait_ge(embT_ready, 2 * t + 2)
                if not (isinstance(t, int) and t < 1):
                    eng.wait_ge(t_full, UNITS * t - UNITS + (UNITS // 2) * (half + 1))
                g = slice(HALF * half, HALF * half + HALF)
                for q in quadrants:
                    part = slice(K * q, K * q + K)
                    last = nc.scalar.copy(diag[part, g, q, 0:F],
                                          embT[n][part, :].rearrange("p (m g) -> p g m", g=GROUPS)[:, g, :])
                if Q - 1 in quadrants:
                    last.then_inc(diag_ready, 1)

            def unit_out(t, n, u):
                if u == 0 and isinstance(t, int) and t == 0:
                    eng.wait_ge(top1_ready, 1)
                if u == 0 and not (isinstance(t, int) and t < 2):
                    eng.wait_ge(z_full, t - 1)
                    eng.wait_ge(packs_ready, t - 1)
                eng.wait_ge(t_full, UNITS * t + u + 1)
                src = psum[0:ROWS, u % T_BANKS, :].rearrange("p (b c) -> p b c", b=UNIT)
                src = src[:, :, 0:Q * 2 * TS].rearrange("p g (q s) -> p g q s", q=Q)
                dst = tsum[0:ROWS, n].rearrange("p s (q g) -> p g q s", q=Q)[:, UNIT * u:UNIT * u + UNIT]
                nc.scalar.copy(dst, src).then_inc(t_out, 1)

            def z_move(t, i, n):
                if not (isinstance(i, int) and i < 1):
                    eng.wait_ge(h1_full, i)
                eng.wait_ge(z_full, t + 1)
                nc.scalar.copy(z_hi[:, 0, n, :], z_ps[:, 0:NP])
                nc.scalar.activation(z_hi[:, 1, n, :], z_ps[:, NP:2 * NP], ACT.Identity, bias=b2k[:, 0:1]).then_inc(z_out, 1)

            def h1_move(t, i, n):
                if not (isinstance(t, int) and t < 2):
                    eng.wait_ge(h2_full, t - 1)
                eng.wait_ge(h1_full, i + 1)
                if n == 1:
                    eng.wait_ge(h1_lo_ready, t)
                nc.scalar.activation(h1_hi[:, n, :].rearrange("p (a b) -> p a b", b=NP), h1_ps[:, :, n, :],
                                     ACT.Relu).then_inc(h1_out, 1)

            def step(t, i, n):
                known = isinstance(t, int)
                if not known or t < TILES:
                    for u in range(UNITS // 2):
                        unit_out(t, n, u)
                if not known or 3 <= t < TILES:
                    h1_move(t - 3, i - 2 + n, 1 - n)
                if not known or t < TILES:
                    for u in range(UNITS // 2, UNITS):
                        unit_out(t, n, u)
                        q = u - UNITS // 2
                        if known and t == 0 and q < Q:
                            fill_diag(1, 1, 0, [q])
                if not known or 1 <= t < TILES - 1:
                    fill_diag(t + 1, 1 - n, 0)
                if not known or t < TILES - 1:
                    fill_diag(t + 1, 1 - n, 1)
                if known and t == 0:
                    eng.wait_ge(top2_ready, 1)
                    eng.wait_ge(dense_ready, 3)
                    nc.scalar.copy(packs[:, 1, :, :].rearrange("p s b -> p (s b)"),
                                   zero[:, :].broadcast_to([NP, NPACK * NP])).then_inc(packs_zero, 1)
                if known and t == TILES - 1:
                    h1_move(t - 2, i - 1, 1)
                if not known or t >= 1:
                    z_move(t - 1, i - 1 + n, 1 - n)

            eng.wait_ge(consts_ready, 1)
            eng.wait_ge(v_zero, 1)
            v_out(AFTER_MOVED, AFTER_V0)
            for half in range(2):
                fill_diag(0, 0, half)
            v_out(AFTER_V0, PREPS)
            for t in range(6):
                step(t, t // 2, t % 2)
            with eng.Fori(3, TILES // 2 - 1) as i:
                for n in range(2):
                    step(2 * i + n, i, n)
            for t in range(TILES - 2, TILES + 1):
                step(t, t // 2, t % 2)
            for n in range(2):
                h1_move(TILES - 2 + n, TILES // 2 - 1, n)

        @block.tensor
        def _(eng):
            def free_bank(n):
                if n >= 4:
                    eng.wait_ge(prep_out, n - 3)

            eng.wait_ge(ident_ready, 1)
            eng.wait_ge(w2_in, 16)
            for n, ms in enumerate(w2T_jobs):
                free_bank(n)
                for a, m in enumerate(ms):
                    last = nc.tensor.transpose(prep_bank(n)[:, a * H:(a + 1) * H], w2raw[:, :, m], ident[:, :])
                last.then_inc(prep_full, 1)
            eng.wait_ge(sym_ready, 1)
            for x in range(F):
                n = AFTER_W2T + x
                eng.wait_ge(prep_out, max(n - 3, x // 4 + 1))
                nc.tensor.matmul(prep_bank(n)[:, 0:(F - x % HF) * HF], w2T[:, x, :],
                                 w1s[x // HF][:, x % HF:F, :].rearrange("p y z -> p (y z)"),
                                 start=True, stop=True).then_inc(prep_full, 1)
            def make_v():
                eng.wait_ge(b1_in, 32)
                for n, (columns, _) in enumerate(v_jobs, AFTER_MOVED):
                    free_bank(n)
                    if n == AFTER_MOVED + JOBS_W1:
                        eng.wait_ge(extra_ready, 1)
                    if n == AFTER_V0:
                        eng.wait_ge(extra_ready, 2)
                    for a, (what, c, third, rows) in enumerate(columns):
                        dst = prep_bank(n)[0:rows, a * H:(a + 1) * H]
                        if what == "one":
                            last = nc.tensor.matmul(dst, w1p[:, c, 0:rows], ident[:, :], start=True, stop=True)
                        elif what == "cross":
                            last = nc.tensor.matmul(dst, w1s[c][:, HF + third, 0:rows], ident[:, :], start=True, stop=True)
                        else:
                            y_local = third + HF * (what == "other")
                            m = HF * c + third if what == "own" else HF * (1 - c) + third
                            nc.tensor.matmul(dst, w1p[:, c, 0:rows], w2T[:, m, :], start=True, stop=False)
                            pr = min(rows, NPAIR)
                            last = nc.tensor.matmul(prep_bank(n)[0:pr, a * H:(a + 1) * H], extra[c][:, y_local, 0:pr],
                                                    ident[:, :], start=False, stop=True)
                    last.then_inc(prep_full, 1)

            def t_units(t, n, half):
                eng.wait_ge(pairs_ready, 2 * t + half + 1)
                eng.wait_ge(diag_ready, 2 * t + half + 1)
                for u in range(half * UNITS // 2, (half + 1) * UNITS // 2):
                    if u == 1 and (not isinstance(t, int) or t + 1 < TILES):
                        short_rows(t + 1)
                    before = u - T_BANKS if u >= T_BANKS else max(w for w in range(UNITS) if w % T_BANKS == u) - UNITS
                    if not (isinstance(t, int) and UNITS * t + before < 0):
                        eng.wait_ge(t_out, UNITS * t + before + 1)
                    for j in range(UNIT):
                        g = UNIT * u + j
                        at = j * (BANK // UNIT)
                        dst = psum[0:ROWS, u % T_BANKS, at:at + Q * 2 * TS]
                        dst = dst.rearrange("p (q s) -> p q s", q=Q)
                        for c in range(2):
                            last = nc.tensor.matmul(dst[:, :, c * TS:(c + 1) * TS], pairs[:, half, g % HALF, c, :],
                                                    diag[:, g, :, :], start=True, stop=True)
                    last.then_inc(t_full, 1)

            def cin(t, n):
                eng.wait_ge(packs_ready, t + 1)
                if isinstance(t, int) and t == 0:
                    eng.wait_ge(prep_out, PREPS)
                else:
                    eng.wait_ge(z_lo_ready, t)
                terms = [(V_ONE, tsum, ONE, 2 * LOW)] + [(V_P1 + a, packs, P1 + a, KP) for a in range(N1S)]
                for a, (s, src, slot, rows) in enumerate(terms):
                    nc.tensor.matmul(z_ps[:, 0:NP], v[0:rows, s, :], src[0:rows, n, slot, :],
                                     start=(a == 0), stop=(a == len(terms) - 1))
                terms = [(V_OTHER + nu, tsum, HF + nu, 2 * LOW) for nu in range(HF)]
                terms += [(V_OWN + mu - SMALL, tsum, mu, 2 * LOW) for mu in range(SMALL, HF)]
                terms += [(V_P28 + a, packs, P28 + a, KP) for a in range(N28)]
                for a, (s, src, slot, rows) in enumerate(terms):
                    last = nc.tensor.matmul(z_ps[:, NP:2 * NP], v[0:rows, s, :], src[0:rows, n, slot, :],
                                            start=(a == 0), stop=(a == len(terms) - 1))
                last.then_inc(z_full, 1)

            def short_rows(t):
                eng.wait_ge(onehot_ready, t)
                if isinstance(t, int) and t == 1:
                    eng.wait_ge(prep_out, PREPS)
                else:
                    eng.wait_ge(rows_ready, t - 1)
                for j in range(SHORTS):
                    for c in range(CHUNKS):
                        last = nc.tensor.matmul(rows_ps[:, j * PARTS * K:(j + 1) * PARTS * K], onehot[:, c, j, :],
                                                table_parts[:, j, c].rearrange("p a k -> p (a k)"),
                                                start=(c == 0), stop=(c == CHUNKS - 1))
                last.then_inc(rows_full, 1)

            def layer1(i):
                if isinstance(i, int) and i == 0:
                    eng.wait_ge(dense_ready, 3)
                    eng.wait_ge(top1_ready, 1)
                else:
                    eng.wait_ge(h1_lo_ready, 2 * i)
                eng.wait_ge(z_out, 2 * i + 2)
                for a in range(N1 // NP):
                    dst = h1_ps[:, a, :, :].rearrange("p n b -> p (n b)")
                    cols = slice(a * NP, (a + 1) * NP)
                    nc.tensor.matmul(dst, top1d[:, cols], denseT[:, bass.ts(i, 2 * NP)], start=True, stop=False)
                    for top1, z in ((top1_hi, z_hi), (top1_lo, z_hi), (top1_hi, z_lo)):
                        if a == 0 and z is z_lo:
                            eng.wait_ge(z_lo_ready, 2 * i + 2)
                        for s in range(2):
                            last = nc.tensor.matmul(dst, top1[:, s, cols], z[:, s, :, :].rearrange("p n b -> p (n b)"),
                                                    start=False, stop=(z is z_lo and s == 1))
                last.then_inc(h1_full, 1)

            def layer2(t, n):
                eng.wait_ge(h1_out, t + 1)
                if isinstance(t, int) and t == 0:
                    eng.wait_ge(top2_ready, 1)
                else:
                    eng.wait_ge(y_ready, t)
                dst = h2_ps[:, 0:N2]
                nc.tensor.matmul(dst, denseT[:, 0:NP], top1d[:, N1:N1 + N2], start=True, stop=False)
                for h1, top2 in ((h1_hi, top2_hi), (h1_hi, top2_lo), (h1_lo, top2_hi)):
                    if h1 is h1_lo:
                        eng.wait_ge(h1_lo_ready, t + 1)
                    for s in range(N1 // NP):
                        last = nc.tensor.matmul(dst, h1[:, n, s * NP:(s + 1) * NP], top2[:, s, :], start=False,
                                                stop=(h1 is h1_lo and s == N1 // NP - 1))
                last.then_inc(h2_full, 1)

            def step(t, i, n):
                known = isinstance(t, int)
                if not known or t < TILES:
                    t_units(t, n, 0)
                if n == 1 and (not known or t >= 3):
                    layer1(i - 1)
                if not known or t < TILES:
                    t_units(t, n, 1)
                if not known or 3 <= t < TILES:
                    layer2(t - 3, 1 - n)
                if not known or t >= 1:
                    cin(t - 1, 1 - n)
                if known and t == TILES - 1:
                    layer2(t - 2, 1)

            eng.wait_ge(consts_ready, 1)
            eng.wait_ge(top_in, 16 * LOADS_TOP)
            make_v()
            for t in range(4):
                step(t, t // 2, t % 2)
            with eng.Fori(2, TILES // 2 - 1) as i:
                for n in range(2):
                    step(2 * i + n, i, n)
            for t in range(TILES - 2, TILES + 1):
                step(t, t // 2, t % 2)
            layer1(TILES // 2 - 1)
            for n in range(2):
                layer2(TILES - 2 + n, n)
            eng.wait_ge(y_ready, TILES)
            nc.tensor.transpose(yT_ps[0:TILES, 0:NP], y[:, :], ident[:, :]).then_inc(yT_full, 1)


def kernel(**inputs):
    import numpy as np
    import concourse.bacc as bacc
    from concourse.bass_utils import run_bass_kernel_spmd

    nc = bacc.Bacc("TRN2", target_bir_lowering=False, num_devices=1)
    arrays = {}

    def dram(name):
        a = np.ascontiguousarray(inputs[name])
        arrays[f"in_{name}"] = a
        return nc.dram_tensor(f"in_{name}", a.shape, mybir.dt.from_np(a.dtype), kind="ExternalInput").ap()

    out = nc.dram_tensor("out_y", (B, 1), fp32, kind="ExternalOutput").ap()
    rows = [inputs[f"tbl_{f}"].shape[0] for f in range(F)]
    inputs["short_ids"] = np.asarray(inputs["ids"])[:, short_fields(rows)].T
    build(nc, dram("dense_ctx"), dram("ids"), dram("short_ids"), [dram(f"tbl_{f}") for f in range(F)],
          dram("W_top1"), dram("b_top1"), dram("W_top2"), dram("b_top2"), dram("W_top3"),
          dram("L0_rec_W1"), dram("L0_rec_b1"), dram("L0_rec_W2"), dram("L0_rec_b2"), out)
    r = run_bass_kernel_spmd(nc, [arrays], core_ids=[0])
    return r.results[0]["out_y"]
```
